# Optimizing a Trainium2 kernel written in Bass

```python
import numpy as np
import jax
import jax.numpy as jnp

def _softmax(x, axis=-1):
    return jax.nn.softmax(x, axis=axis)

def _gelu(x):
    return jax.nn.gelu(x, approximate=True)

def _silu(x):
    return jax.nn.silu(x)

def _sigmoid(x):
    return jax.nn.sigmoid(x)

def _layernorm(x, axis=-1, eps=1e-05):
    m = jnp.mean(x, axis=axis, keepdims=True)
    v = jnp.var(x, axis=axis, keepdims=True)
    return (x - m) / jnp.sqrt(v + eps)

def _scatter_add(tgt, idx, src, axis=0):
    return tgt.at[idx].add(src)

def _segment_sum(src, seg, n):
    return jax.ops.segment_sum(src, seg, n)
kernel_name = 'mk_xattn_ffn_d1_seqx_r4_00892d'

def setup_inputs(seed: int=0):
    np.random.seed(seed)
    _w = jnp.asarray

    def _rec_inputs():
        import jax
        import jax.numpy as jnp
        _rk = jax.random.key(seed)
        x = -0.0003929 + 0.9999 * jax.random.normal(jax.random.fold_in(_rk, 1), (16, 128, 1024), jnp.float32)
        _lenS = 128 - jax.random.randint(jax.random.fold_in(_rk, 7), (16,), 0, max(1, 128 // 4) + 1, jnp.int32)
        _lenS2 = 128 - jax.random.randint(jax.random.fold_in(_rk, 8), (16,), 0, max(1, 128 // 4) + 1, jnp.int32)
        _ctx_4096P = jax.random.normal(jax.random.fold_in(_rk, 11), (16, 16, 1024), jnp.float32)
        _ctx_4096c = jax.random.dirichlet(jax.random.fold_in(_rk, 511), 0.3 * jnp.ones((16,), jnp.float32), (16, 128))
        _ctx_4096t = jnp.einsum('bsk,bkd->bsd', _ctx_4096c, _ctx_4096P)
        _ctx_4096t = _ctx_4096t * jax.lax.rsqrt(jnp.mean(jnp.square(_ctx_4096t)) + 1e-12) * 0.953939
        ctx_4096 = 2.81802e-05 + 1.00001 * (_ctx_4096t + 0.3 * jax.random.normal(jax.random.fold_in(_rk, 611), (16, 128, 1024), jnp.float32))
        return (x, ctx_4096)
    x, ctx_4096 = _rec_inputs()

    def _L0_xattn_setup():
        import jax, jax.numpy as jnp
        import numpy as np
        EMBED = 1024
        NUM_Q = 32
        NUM_KV = 8
        GROUPS = NUM_Q // NUM_KV
        HEAD_DIM = EMBED // NUM_Q
        KV_DIM = HEAD_DIM * NUM_KV
        key = jax.random.key(seed)
        ks = jax.random.split(key, 12)
        B, S = (2, 512)
        s = 0.02
        return {'query': jax.random.normal(ks[0], (B, S, EMBED), jnp.float32), 'key': jax.random.normal(ks[1], (B, S, EMBED), jnp.float32), 'value': jax.random.normal(ks[2], (B, S, EMBED), jnp.float32), 'Wq': jax.random.normal(ks[3], (EMBED, EMBED), jnp.float32) * s, 'bq': jnp.zeros((EMBED,), jnp.float32), 'Wk': jax.random.normal(ks[4], (EMBED, KV_DIM), jnp.float32) * s, 'bk': jnp.zeros((KV_DIM,), jnp.float32), 'Wv': jax.random.normal(ks[5], (EMBED, KV_DIM), jnp.float32) * s, 'bv': jnp.zeros((KV_DIM,), jnp.float32), 'Wo': jax.random.normal(ks[6], (EMBED, EMBED), jnp.float32) * s, 'bo': jnp.zeros((EMBED,), jnp.float32)}
    _L0_xattn_all = _L0_xattn_setup()
    _L0_xattn_in = {k: v for k, v in _L0_xattn_all.items() if k in ('Wq', 'bq', 'Wk', 'bk', 'Wv', 'bv', 'Wo', 'bo')}
    del _L0_xattn_all

    def _L0_ffn_setup():
        import jax, jax.numpy as jnp
        import numpy as np
        import math
        P = 0.8
        key = jax.random.key(seed)
        k1, k2 = jax.random.split(key)
        B, S, IN_DIM, FEATURES = (4, 512, 1024, 1024)
        x = jax.random.normal(k1, (B, S, IN_DIM), dtype=jnp.float32)
        kernel = jax.random.bernoulli(k2, 0.1, (IN_DIM, FEATURES))
        scale = jnp.asarray(1.0 / math.sqrt(IN_DIM), dtype=jnp.float32)
        return {'x': x, 'kernel': kernel, 'scale': scale}
    _L0_ffn_all = _L0_ffn_setup()
    _L0_ffn_in = {k: v for k, v in _L0_ffn_all.items() if k in ('kernel', 'scale')}
    del _L0_ffn_all
    return {'x': x, 'ctx_4096': ctx_4096, 'L0_xattn_Wq': _L0_xattn_in['Wq'], 'L0_xattn_bq': _L0_xattn_in['bq'], 'L0_xattn_Wk': _L0_xattn_in['Wk'], 'L0_xattn_bk': _L0_xattn_in['bk'], 'L0_xattn_Wv': _L0_xattn_in['Wv'], 'L0_xattn_bv': _L0_xattn_in['bv'], 'L0_xattn_Wo': _L0_xattn_in['Wo'], 'L0_xattn_bo': _L0_xattn_in['bo'], 'L0_ffn_kernel': _L0_ffn_in['kernel'], 'L0_ffn_scale': _L0_ffn_in['scale']}

def reference(x, ctx_4096, L0_xattn_Wq, L0_xattn_bq, L0_xattn_Wk, L0_xattn_bk, L0_xattn_Wv, L0_xattn_bv, L0_xattn_Wo, L0_xattn_bo, L0_ffn_kernel, L0_ffn_scale):
    import jax
    import jax.numpy as jnp

    def _L0_xattn_ref(query, key, value, Wq, bq, Wk, bk, Wv, bv, Wo, bo):
        import jax, jax.numpy as jnp
        import numpy as np
        EMBED = 1024
        NUM_Q = 32
        NUM_KV = 8
        GROUPS = NUM_Q // NUM_KV
        HEAD_DIM = EMBED // NUM_Q
        KV_DIM = HEAD_DIM * NUM_KV
        B, S, _ = query.shape
        Q = query @ Wq + bq
        K = key @ Wk + bk
        V = value @ Wv + bv
        Q = Q.reshape(B, S, NUM_KV, GROUPS, HEAD_DIM).transpose(0, 2, 3, 1, 4)
        K = K.reshape(B, S, NUM_KV, HEAD_DIM).transpose(0, 2, 1, 3)
        V = V.reshape(B, S, NUM_KV, HEAD_DIM).transpose(0, 2, 1, 3)
        scale = 1.0 / jnp.sqrt(jnp.asarray(HEAD_DIM, query.dtype))
        scores = jnp.einsum('bhgqd,bhkd->bhgqk', Q, K) * scale
        w = jax.nn.softmax(scores, axis=-1)
        y = jnp.einsum('bhgqk,bhkd->bhgqd', w, V)
        y = y.transpose(0, 3, 1, 2, 4).reshape(B, S, EMBED)
        return y @ Wo + bo

    def _L0_ffn_ref(x, kernel, scale):
        import jax, jax.numpy as jnp
        import numpy as np
        import math
        P = 0.8
        in_dim = x.shape[-1]
        num_excitatory = round(in_dim * P)
        x_exc = x[..., :num_excitatory]
        x_inh = x[..., num_excitatory:]
        x_ei = jnp.concatenate([x_exc, -P / (1.0 - P) * x_inh], axis=-1)
        out = jnp.einsum('bsi,if->bsf', x_ei, kernel.astype(x_ei.dtype))
        return scale * out
    x = x + _L0_xattn_ref(_layernorm(x, axis=-1), ctx_4096, ctx_4096, L0_xattn_Wq, L0_xattn_bq, L0_xattn_Wk, L0_xattn_bk, L0_xattn_Wv, L0_xattn_bv, L0_xattn_Wo, L0_xattn_bo)
    x = x + _L0_ffn_ref(_layernorm(x, axis=-1), L0_ffn_kernel, L0_ffn_scale)
    return x

_drawn_inputs = setup_inputs


def setup_inputs(seed=0):
    import zlib

    import numpy as np

    out = dict(_drawn_inputs(seed))
    spreads = {'L0_xattn_bq': (0.0, 0.8),
     'L0_xattn_bk': (0.0, 0.8),
     'L0_xattn_bv': (0.0, 0.1),
     'L0_xattn_bo': (0.0, 0.1)}
    factors = {}
    for name, (base, spread) in spreads.items():
        noise = np.random.default_rng([zlib.crc32(name.encode()), seed]).standard_normal(out[name].shape)
        drawn = base * np.exp(spread * noise) if base else spread * noise
        out[name] = jnp.asarray(drawn.astype(out[name].dtype))
    for name, factor in factors.items():
        out[name] = (out[name] * factor).astype(out[name].dtype)
    return out
```

```python
import concourse.bass as bass
from concourse import mybir

F32 = mybir.dt.float32
F32R = mybir.dt.float32r
F16 = mybir.dt.float16
U8 = mybir.dt.uint8
ALU = mybir.AluOpType
ACT = mybir.ActivationFunctionType
AX = mybir.AxisListType.X

P = 128
N_BATCH = 16
D = 1024
KC = D // P
BLK = 512
N_BLK = N_BATCH * P // BLK
TPB = BLK // P
HD = 32
NKV = 8
G = 4
KV = NKV * HD
HI, LO = 0, 1
EPS = 1e-5
SOFTMAX_SCALE = float(HD) ** -0.5
P_EXC = 0.8
N_EXC = round(D * P_EXC)
INHIBIT = -4.0
FFN_UP = 256.0
WRING = 3
CRING = 4
XRING = 4
KB = 1024


def wait(engine, semaphore, count):
    if isinstance(count, int) and count <= 0:
        return
    engine.wait_ge(semaphore, count)


def attention_ffn(nc, x, ctx_t, wq, bq, wkv, bk, bv, wo, bo, ffn_w, ffn_scale, out):
    base = (nc.sbuf_base + 31) // 32 * 32
    R_KV = base
    R_Q = R_KV + 32 * KB
    R_A1 = R_Q + 64 * KB
    R_A0 = R_A1 + 32 * KB
    R_W = R_A0 + 32 * KB
    R_C = R_W + WRING * 4 * KB
    R_O = R_C + CRING * 2 * KB
    R_S = R_O + 8 * KB
    R_END = R_S + 9 * KB

    def at(name, shape, dtype, offset):
        return nc.alloc_sbuf_tensor_at(name, shape, dtype, offset=offset)

    cursor = [R_END]

    def const(name, shape, dtype):
        size = 4
        for s in shape[1:]:
            size *= s
        t = at(name, shape, dtype, cursor[0])
        cursor[0] += (size + 31) // 32 * 32
        return t

    wkv_s = at("wkv_s", [P, KC, 2, 2 * KV], F32R, R_KV)
    wq_s = at("wq_s", [P, KC, 2, D], F32R, R_Q)
    act = [at(f"act{i}", [P, KC, 2, BLK], F32R, r) for i, r in ((0, R_A0), (1, R_A1))]
    w_raw = [at(f"w_raw{i}", [P, D], F32, R_W + i * 4 * KB) for i in range(WRING)]
    c_raw = [at(f"c_raw{i}", [P, BLK], F32, R_C + i * 2 * KB) for i in range(CRING)]
    x_raw = [at(f"x_raw{i}", [P, D], F32, R_W + i * 4 * KB if i < WRING else R_S + 4 * KB)
             for i in range(XRING)]
    proj = [at(f"proj{i}", [P, TPB, 2, P], F32R, R_O + i * 4 * KB) for i in range(2)]
    v_out = at("v_out", [P, TPB, KV], F32, R_S)
    wo_lo4 = at("wo_lo4", [P, KC // 2, 2, D], F32R, R_KV)
    wo_hi4 = at("wo_hi4", [P, KC // 2, 2, D], F32R, R_Q)
    ffn_s = at("ffn_s", [P, KC, D], F16, R_Q + 32 * KB)
    x_in = [at(f"x_in{i}", [P, D], F32, R_Q + (48 + 4 * i) * KB) for i in range(2)]
    x2 = [at(f"x2_{i}", [P, D], F32, R_Q + (56 + 4 * i) * KB) for i in range(2)]
    kd = at("kd", [P, NKV, 2, G * P], F32R, R_A1)
    pr = [at(f"pr{i}", [P, G, P], F32, R_A0 + i * 2 * KB) for i in range(2)]
    pt = at("pt", [P, NKV, G * P], F32, R_A0 + 4 * KB)
    yt = at("yt", [P, KC, 2, P], F32R, R_A0 + 20 * KB)
    xn2 = at("xn2", [P, D], F32, R_A0 + 28 * KB)
    xnt = [at(f"xnt{i}", [P, 2, KC, P], F16, R_W + i * 4 * KB) for i in range(2)]
    wo_raw = [at(f"wo_raw{i}", [P, D], F32, R_C + i * 4 * KB) for i in range(2)]
    ffn_raw = at("ffn_raw", [P, KC, D], U8, R_C)
    q_s = [at("q_s0", [P, NKV, 2, P], F32R, R_S), at("q_s1", [P, NKV, 2, P], F32R, R_O)]
    v_s = [at("v_s0", [P, KV], F32, R_S + 8 * KB), const("v_s1", [P, KV], F32)]
    ident = const("ident", [P, P], F32)
    ffn_sign = const("ffn_sign", [P, KC], F32)
    bq_s = const("bq_s", [P, KC], F32)
    bk_s = const("bk_s", [P, 2], F32)
    bv_s = const("bv_s", [P, KV], F32)
    bo_s = const("bo_s", [P, D], F32)
    scale_s = const("scale_s", [P, 1], F32)
    scale_d = const("scale_d", [P, 1], F32)
    minus_half = const("minus_half", [P, 1], F32)
    eps_s = const("eps_s", [P, 1], F32)
    st = const("st", [P, 2, 6], F32)
    mv = [const(f"mv{i}", [P, 2], F32) for i in range(2)]
    ve = const("ve", [P, 1], F32)
    rstd = [const(f"rstd{i}", [P, 1], F32) for i in range(2)]
    mx = [const(f"mx{i}", [P, G], F32) for i in range(2)]
    nb = [const(f"nb{i}", [P, G], F32) for i in range(2)]
    sums = [const(f"sums{i}", [P, G], F32) for i in range(2)]
    rsum = [const(f"rsum{i}", [P, G], F32) for i in range(2)]
    assert cursor[0] <= nc.sbuf_usable_end, (cursor[0], nc.sbuf_usable_end)

    bank = [nc.alloc_psum_tensor(f"bank{i}", [P, 512], F32) for i in range(8)]
    score, prob_t, x_t = bank[4:6], bank[6:8], bank[6:8]
    y_bank, xt3 = bank[2], bank[3]

    q_d = nc.dram_tensor("q_d", [N_BATCH, P, NKV, 2, P], F32)
    k_d = nc.dram_tensor("k_d", [N_BATCH, HD, NKV, 2, P], F32)
    v_d = nc.dram_tensor("v_d", [N_BATCH, P, KV], F32)

    S = {n: nc.alloc_semaphore(n) for n in (
        "const_loaded", "const_made", "c_loaded0", "c_loaded1", "c_loaded2", "c_loaded3",
        "wkv_loaded0", "wkv_loaded1", "wkv_loaded2",
        "wkv_hi", "wkv_ready", "c_hi", "c_ready", "c_used", "kv_done", "k_hi", "kv_evac",
        "k_stored", "v_stored", "wq_loaded0", "wq_loaded1", "wq_loaded2", "wq_hi", "wq_ready",
        "x_loaded0", "x_loaded1", "x_loaded2", "x_loaded3", "ln_step", "ln_var", "ln_ve",
        "ln_rstd", "xn_ready", "xt_done", "xt_hi", "xt_ready", "q_done", "q_hi", "q_evac",
        "q_stored0", "q_stored1", "wo_loaded0", "wo_loaded1", "wo_hi", "wo_ready",
        "ffn_loaded", "ffn_ready", "kd_zeroed",
        "kd_loaded0", "kd_loaded1", "qv_loaded0", "qv_loaded1", "x_in_loaded0", "x_in_loaded1",
        "qk_done", "max_done", "neg_max_ready", "exp_done", "rsum_ready", "prob_ready", "tp_done",
        "pt_ready", "pv_done", "y_hi", "y_ready", "xbo_ready", "o_done", "x2_ready",
        "xn2_ready", "x2t_done", "x2t_hi", "x2t_ready", "ffn_done", "out_ready",
        "out_stored0", "out_stored1")}
    (const_loaded, const_made, wkv_hi, wkv_ready, c_hi, c_ready, c_used, kv_done, k_hi, kv_evac,
     k_stored, v_stored, wq_hi, wq_ready, ln_step, ln_var, ln_ve, ln_rstd, xn_ready, xt_done,
     xt_hi, xt_ready, q_done, q_hi, q_evac, wo_hi, wo_ready, ffn_loaded, ffn_ready, kd_zeroed,
     qk_done, max_done, neg_max_ready, exp_done, rsum_ready, prob_ready, tp_done, pt_ready,
     pv_done, y_hi, y_ready, xbo_ready, o_done, x2_ready, xn2_ready, x2t_done, x2t_hi,
     x2t_ready, ffn_done, out_ready) = (S[n] for n in (
         "const_loaded", "const_made", "wkv_hi", "wkv_ready", "c_hi", "c_ready", "c_used",
         "kv_done", "k_hi", "kv_evac", "k_stored", "v_stored", "wq_hi", "wq_ready", "ln_step",
         "ln_var", "ln_ve", "ln_rstd", "xn_ready", "xt_done", "xt_hi", "xt_ready", "q_done",
         "q_hi", "q_evac", "wo_hi", "wo_ready", "ffn_loaded", "ffn_ready", "kd_zeroed",
         "qk_done", "max_done", "neg_max_ready", "exp_done", "rsum_ready", "prob_ready",
         "tp_done", "pt_ready", "pv_done", "y_hi", "y_ready", "xbo_ready", "o_done", "x2_ready",
         "xn2_ready", "x2t_done", "x2t_hi", "x2t_ready", "ffn_done", "out_ready"))
    c_loaded = [S[f"c_loaded{i}"] for i in range(CRING)]
    wkv_loaded = [S[f"wkv_loaded{i}"] for i in range(WRING)]
    wq_loaded = [S[f"wq_loaded{i}"] for i in range(WRING)]
    x_loaded = [S[f"x_loaded{i}"] for i in range(XRING)]
    wo_loaded = [S["wo_loaded0"], S["wo_loaded1"]]
    q_stored = [S["q_stored0"], S["q_stored1"]]
    kd_loaded = [S["kd_loaded0"], S["kd_loaded1"]]
    qv_loaded = [S["qv_loaded0"], S["qv_loaded1"]]
    x_in_loaded = [S["x_in_loaded0"], S["x_in_loaded1"]]
    out_stored = [S["out_stored0"], S["out_stored1"]]

    N_CONST_DMA = 5
    N_TILE = N_BATCH
    block = nc.Block()

    def wo_chunk(kk, part):
        half = wo_lo4 if kk < KC // 2 else wo_hi4
        return half[:, kk % (KC // 2), part, :]

    def act_of(n):
        return act[(n + 1) % 2]

    with block:

        @block.sync
        def _(sp):
            def load_c(n, k):
                wait(sp, c_ready, KC * n + k + 1 - CRING)
                sp.dma_start(c_raw[k % CRING][:, :],
                             ctx_t[k * P:(k + 1) * P, bass.ds(n * BLK, BLK)]).then_inc(c_loaded[k % CRING], 16)

            def store_kv(n):
                for j in range(2):
                    wait(sp, kv_evac, 6 * n + j + 1)
                    for c in range(4):
                        sp.dma_start(
                            k_d[bass.ds(n * TPB, TPB), :, 4 * j + c, :, :].rearrange("b d h t -> d b (h t)"),
                            proj[j][c * HD:(c + 1) * HD, :, :, :].rearrange("d b h t -> d b (h t)").bitcast(F32),
                        ).then_inc(k_stored, 16)
                wait(sp, kv_evac, 6 * n + 6)
                sp.dma_start(v_d[bass.ds(n * TPB, TPB), :, :].rearrange("b p v -> p b v"),
                             v_out[:, :, :]).then_inc(v_stored, 16)

            for k in range(KC):
                load_c(0, k)
                wait(sp, wkv_ready, k + 1 - WRING)
                sp.dma_start(w_raw[k % WRING][:, 0:2 * KV],
                             wkv[k * P:(k + 1) * P, :]).then_inc(wkv_loaded[k % WRING], 16)
                if k == 1:
                    sp.dma_start(bq_s[:, :], bq).then_inc(const_loaded, 16)
                    sp.dma_start(bk_s[:, :], bk).then_inc(const_loaded, 16)
                    sp.dma_start(bv_s[:, :], bv.partition_broadcast(P)).then_inc(const_loaded, 16)
                    sp.dma_start(bo_s[:, :], bo.partition_broadcast(P)).then_inc(const_loaded, 16)
                    sp.dma_start(scale_s[:, :], ffn_scale.partition_broadcast(P)).then_inc(const_loaded, 16)
            with sp.Fori(1, N_BLK) as n:
                for k in range(KC):
                    load_c(n, k)
                store_kv(n - 1)
            def load_x(i):
                wait(sp, xt_done, 2 * (i - XRING + 1))
                sp.dma_start(x_raw[i % XRING][:, :],
                             x[i * P:(i + 1) * P, :]).then_inc(x_loaded[i % XRING], 16)

            wait(sp, wq_ready, KC)
            for i in range(3):
                load_x(i)
            store_kv(N_BLK - 1)
            wait(sp, v_stored, 16 * N_BLK)
            for i in range(3, 2 * XRING):
                load_x(i)

            def store_q(n, m):
                wait(sp, q_evac, NKV * n + m + 1)
                sp.dma_start(
                    q_d[n * TPB:(n + 1) * TPB, :, m, :, :].rearrange("b p h t -> p b (h t)"),
                    proj[m % 2][:, :, :, :].rearrange("p b h t -> p b (h t)").bitcast(F32),
                ).then_inc(q_stored[m % 2], 16)

            def load_kd(b, half):
                for g in range(G):
                    sp.dma_start(
                        kd[g * HD:(g + 1) * HD, 4 * half:4 * half + 4, :, g * P:(g + 1) * P]
                        .rearrange("p c h t -> p (c h) t").bitcast(F32),
                        k_d[b, :, 4 * half:4 * half + 4, :, :].rearrange("d c h t -> d (c h) t"),
                    ).then_inc(kd_loaded[half], 16)

            def load_qv(b, par):
                sp.dma_start(q_s[par][:, :, :, :].rearrange("p c h t -> p (c h t)").bitcast(F32),
                             q_d[b].rearrange("p c h t -> p (c h t)")).then_inc(qv_loaded[par], 16)
                sp.dma_start(v_s[par][:, :], v_d[b]).then_inc(qv_loaded[par], 16)

            for n in range(N_BLK):
                for m in range(NKV):
                    store_q(n, m)
                    if m % 2 == 0 and n < N_BLK - 2:
                        load_x(4 * (n + 2) + m // 2)
                    if n == N_BLK - 1 and m == 1:
                        wait(sp, k_stored, 8 * 16 * N_BLK)
                        wait(sp, q_stored[0], 16 * 4)
                        wait(sp, q_stored[1], 16 * 4)
                        wait(sp, kd_zeroed, 1)
                        wait(sp, xt_done, 2 * N_TILE)
                        load_kd(0, 0)
                        load_kd(0, 1)
                        load_qv(0, 0)
            wait(sp, q_stored[0], 16 * 4 * N_BLK)
            wait(sp, q_stored[1], 16 * 4 * N_BLK)
            wait(sp, q_done, NKV * N_BLK)

            def step(b, i, par, attn, tail2):
                if attn:
                    wait(sp, x2_ready, 2 * (b - 2) + 2)
                    sp.dma_start(x_in[par][:, :], x[bass.ds(b * P, P), :]).then_inc(x_in_loaded[par], 16)
                if attn != "last":
                    if attn:
                        wait(sp, pv_done, 2 * b)
                        load_qv(b + 1, 1 - par)
                        wait(sp, qk_done, NKV * b + 4)
                        load_kd(b + 1, 0)
                if tail2:
                    wait(sp, out_ready, 2 * (b - 2) + 2)
                    sp.dma_start(out[bass.ds((b - 2) * P, P), :], x2[par][:, :]).then_inc(out_stored[par], 16)
                if attn and attn != "last":
                    wait(sp, qk_done, NKV * b + 8)
                    load_kd(b + 1, 1)

            step(0, 0, 0, True, False)
            step(1, 0, 1, True, False)
            step(2, 1, 0, True, True)
            step(3, 1, 1, True, True)
            with sp.Fori(2, N_BATCH // 2 - 1) as i:
                step(2 * i, i, 0, True, True)
                step(2 * i + 1, i, 1, True, True)
            last = N_BATCH // 2 - 1
            step(2 * last, last, 0, True, True)
            step(2 * last + 1, last, 1, "last", True)
            step(N_BATCH, last + 1, 0, False, True)
            step(N_BATCH + 1, last + 1, 1, False, True)
            wait(sp, out_stored[0], 16 * N_BATCH // 2)
            wait(sp, out_stored[1], 16 * N_BATCH // 2)

        @block.gpsimd
        def _(pool):
            pool.memset(ident[:, :], 0.0).then_inc(const_made, 1)
            pool.memset(ffn_sign[:, :], 1.0).then_inc(const_made, 1)
            pool.memset(minus_half[:, :], -0.5).then_inc(const_made, 1)
            pool.memset(eps_s[:, :], EPS).then_inc(const_made, 1)
            pool.wait_ge(const_made, 4)
            pool.affine_select(out=ident[:, :], in_=ident[:, :], compare_op=ALU.not_equal, fill=1.0,
                               base=0, pattern=[[-1, P]], channel_multiplier=1).then_inc(const_made, 1)
            pool.affine_select(out=ffn_sign[:, :], in_=ffn_sign[:, :], compare_op=ALU.is_ge, fill=INHIBIT,
                               base=N_EXC - 1, pattern=[[-P, KC]], channel_multiplier=-1).then_inc(const_made, 1)
            pool.wait_ge(const_made, 6)
            pool.wait_ge(const_loaded, 16 * N_CONST_DMA)
            pool.tensor_scalar(scale_d[:, :], scale_s[:, :], 1.0 / FFN_UP, None, ALU.mult).then_inc(const_made, 1)

            def load_wq(k):
                if k < WRING:
                    pool.wait_ge(wkv_ready, KC)
                else:
                    pool.wait_ge(wq_ready, k - WRING + 1)
                pool.dma_start(w_raw[k % WRING][:, :], wq[k * P:(k + 1) * P, :]).then_inc(wq_loaded[k % WRING], 16)

            for k in range(WRING - 1):
                load_wq(k)
            for k in range(KC):
                if k + WRING - 1 < KC:
                    load_wq(k + WRING - 1)
                pool.wait_ge(wq_loaded[k % WRING], 16 * (k // WRING + 1))
                pool.tensor_copy(wq_s[:, k, HI, :], w_raw[k % WRING][:, :]).then_inc(wq_hi, 1)
                pool.wait_ge(wq_hi, k + 1)
                pool.tensor_tensor(wq_s[:, k, LO, :], w_raw[k % WRING][:, :], wq_s[:, k, HI, :].bitcast(F32),
                                   ALU.subtract).then_inc(wq_ready, 1)

            def inv_std(i, par):
                wait(pool, ln_var, i + 1)
                pool.tensor_tensor(ve[:, :], mv[par][:, 1:2], eps_s[:, :], ALU.add).then_inc(ln_ve, 1)
                wait(pool, ln_ve, i + 1)
                pool.tensor_tensor(rstd[par][:, :], ve[:, :], minus_half[:, :], ALU.pow).then_inc(ln_rstd, 1)

            def load_wo(k):
                if k < 2:
                    pool.wait_ge(c_ready, KC * N_BLK)
                else:
                    pool.wait_ge(wo_ready, k - 1)
                pool.dma_start(wo_raw[k % 2][:, :], wo[k * P:(k + 1) * P, :]).then_inc(wo_loaded[k % 2], 16)

            def split_wo(k):
                pool.wait_ge(wo_loaded[k % 2], 16 * (k // 2 + 1))
                if k == 0:
                    pool.wait_ge(kv_done, 6 * N_BLK)
                if k == KC // 2:
                    pool.wait_ge(q_done, NKV * N_BLK)
                pool.tensor_copy(wo_chunk(k, HI), wo_raw[k % 2][:, :]).then_inc(wo_hi, 1)
                pool.wait_ge(wo_hi, k + 1)
                pool.tensor_tensor(wo_chunk(k, LO), wo_raw[k % 2][:, :], wo_chunk(k, HI).bitcast(F32),
                                   ALU.subtract).then_inc(wo_ready, 1)
                if k + 2 < KC:
                    load_wo(k + 2)

            for i in range(5):
                inv_std(i, i % 2)
            load_wo(0)
            load_wo(1)
            for i in range(5, N_TILE):
                if i - 5 < KC // 2:
                    split_wo(i - 5)
                inv_std(i, i % 2)
            pool.wait_ge(q_done, NKV * (N_BLK - 1))
            pool.memset(kd[:, :, :, :].rearrange("p a b c -> p (a b c)").bitcast(F32), 0.0).then_inc(kd_zeroed, 1)

            def add_bo(b, i, par):
                wait(pool, x_in_loaded[par], 16 * (i + 1))
                pool.tensor_tensor(x_in[par][:, :], x_in[par][:, :], bo_s[:, :], ALU.add).then_inc(xbo_ready, 1)

            for k in range(KC // 2, KC):
                split_wo(k)
            add_bo(0, 0, 0)
            add_bo(1, 0, 1)
            pool.wait_ge(wo_ready, KC)
            pool.dma_start(ffn_raw[:, :, :], ffn_w.rearrange("(k p) n -> p k n", p=P)).then_inc(ffn_loaded, 16)
            pool.wait_ge(ffn_loaded, 16)
            for k in range(KC):
                pool.tensor_scalar(ffn_s[:, k, :], ffn_raw[:, k, :], ffn_sign[:, k:k + 1], None,
                                   ALU.mult).then_inc(ffn_ready, 1)
            inv_std(N_TILE, 0)
            with pool.Fori(1, N_BATCH // 2) as i:
                add_bo(2 * i, i, 0)
                inv_std(N_TILE + 2 * i - 1, 1)
                add_bo(2 * i + 1, i, 1)
                inv_std(N_TILE + 2 * i, 0)
            inv_std(N_TILE + N_BATCH - 1, 1)

        @block.scalar
        def _(sc):
            def c_split(n, k):
                wait(sc, c_loaded[k % CRING], 16 * (2 * n + k // CRING + 1))
                if k < KC - 1:
                    wait(sc, c_used, (KC - 1) * (n - 1) + k + 1)
                else:
                    wait(sc, kv_done, 6 * n)
                sc.activation(act[0][:, k, HI, :], c_raw[k % CRING][:, :], ACT.Copy).then_inc(c_hi, 1)

            def k_evac(n):
                for j in range(2):
                    wait(sc, kv_done, 6 * n + j + 1)
                    wait(sc, k_stored, 8 * 16 * n)
                    sc.activation(proj[j][:, :, HI, :], bank[j][:, :].rearrange("p (b t) -> p b t", b=TPB),
                                  ACT.Identity, bias=bk_s[:, j:j + 1]).then_inc(k_hi, 1)

            for k in range(KC):
                c_split(0, k)
                sc.wait_ge(wkv_loaded[k % WRING], 16 * (k // WRING + 1))
                sc.activation(wkv_s[:, k, HI, :], w_raw[k % WRING][:, 0:2 * KV], ACT.Copy).then_inc(wkv_hi, 1)
            sc.wait_ge(const_loaded, 16 * N_CONST_DMA)

            def kv_block(n):
                for k in range(2):
                    c_split(n, k)
                k_evac(n - 1)
                for k in range(2, KC):
                    c_split(n, k)

            kv_block(1)
            with sc.Fori(2, N_BLK) as n:
                kv_block(n)
            k_evac(N_BLK - 1)

            def xt_evac(i):
                n, t = i // TPB, i % TPB
                for r in range(2):
                    wait(sc, xt_done, 2 * i + r + 1)
                    wait(sc, q_done, NKV * (n - 1))
                    sc.activation(act_of(n)[:, 4 * r:4 * r + 4, HI, t * P:(t + 1) * P],
                                  x_t[r][:, :].rearrange("p (k t) -> p k t", k=4), ACT.Copy).then_inc(xt_hi, 1)

            for i in range(TPB):
                xt_evac(i)
            for n in range(N_BLK):
                for m in range(NKV):
                    wait(sc, q_done, NKV * n + m + 1)
                    if n == 0:
                        wait(sc, k_stored, 8 * 16 * N_BLK)
                    wait(sc, q_stored[m % 2], 16 * (4 * n + m // 2))
                    sc.activation(proj[m % 2][:, :, HI, :], bank[m % 4][:, :].rearrange("p (b t) -> p b t", b=TPB),
                                  ACT.Identity, bias=bq_s[:, m:m + 1]).then_inc(q_hi, 1)
                    if m % 2 == 0 and n < N_BLK - 1:
                        xt_evac(TPB * (n + 1) + m // 2)

            def exps(b, u):
                par = u % 2
                wait(sc, neg_max_ready, NKV * b + u + 1)
                wait(sc, tp_done, NKV * b + u - 1)
                for g in range(G):
                    last = sc.activation(pr[par][:, g, :], score[par][:, g * P:(g + 1) * P], ACT.Exp,
                                         bias=nb[par][:, g:g + 1], scale=SOFTMAX_SCALE,
                                         accum_out=sums[par][:, g:g + 1])
                last.then_inc(exp_done, 1)

            def pt_evac(b, u):
                wait(sc, tp_done, NKV * b + u + 1)
                wait(sc, pv_done, 2 * (b - 1) + u // 4 + 1)
                sc.activation(pt[:, u, :], prob_t[u % 2][:, :], ACT.Copy).then_inc(pt_ready, 1)

            def y_evac(b, half):
                wait(sc, pv_done, 2 * b + half + 1)
                wait(sc, o_done, 2 * b)
                sc.activation(yt[:, 4 * half:4 * half + 4, HI, :],
                              y_bank[:, :].rearrange("p (g q) -> p g q", g=G), ACT.Copy).then_inc(y_hi, 1)

            def x2t_evac(b, par, r):
                wait(sc, x2t_done, 2 * b + r + 1)
                if r == 0:
                    wait(sc, ffn_done, 2 * (b - 2) + 2)
                sc.activation(xnt[par][:, HI, 4 * r:4 * r + 4, :],
                              xt3[:, :].rearrange("p (k t) -> p k t", k=4), ACT.Copy,
                              scale=FFN_UP).then_inc(x2t_hi, 1)

            def step(b, par, attn, tail1, tail2):
                for u in range(NKV):
                    if attn:
                        exps(b, u)
                    if u == 0:
                        if tail2:
                            x2t_evac(b - 2, par, 1)
                        if tail1:
                            pt_evac(b - 1, 7)
                            y_evac(b - 1, 1)
                    elif attn:
                        pt_evac(b, u - 1)
                    if u == 5 and attn:
                        y_evac(b, 0)
                    if u == 7 and tail1:
                        x2t_evac(b - 1, 1 - par, 0)

            step(0, 0, True, False, False)
            step(1, 1, True, True, False)
            step(2, 0, True, True, True)
            step(3, 1, True, True, True)
            with sc.Fori(2, N_BATCH // 2) as i:
                step(2 * i, 0, True, True, True)
                step(2 * i + 1, 1, True, True, True)
            step(N_BATCH, 0, False, True, True)
            step(N_BATCH + 1, 1, False, False, True)

        @block.vector
        def _(dve):
            def c_split(n, k):
                wait(dve, c_hi, KC * n + k + 1)
                dve.tensor_tensor(act[0][:, k, LO, :], c_raw[k % CRING][:, :], act[0][:, k, HI, :].bitcast(F32),
                                  ALU.subtract).then_inc(c_ready, 1)

            def kv_out(n):
                for j in range(2):
                    wait(dve, k_hi, 2 * n + j + 1)
                    dve.scalar_tensor_tensor(
                        out=proj[j][:, :, LO, :], in0=bank[j][:, :].rearrange("p (b t) -> p b t", b=TPB),
                        scalar=bk_s[:, j:j + 1], in1=proj[j][:, :, HI, :].bitcast(F32),
                        op0=ALU.add, op1=ALU.subtract).then_inc(kv_evac, 1)
                for t in range(TPB):
                    wait(dve, kv_done, 6 * n + 3 + t)
                    wait(dve, v_stored, 16 * n)
                    dve.tensor_tensor(v_out[:, t, :], bank[2 + t][:, 0:KV], bv_s[:, :],
                                      ALU.add).then_inc(kv_evac, 1)

            for k in range(KC):
                c_split(0, k)
                wait(dve, wkv_hi, k + 1)
                dve.tensor_tensor(wkv_s[:, k, LO, :], w_raw[k % WRING][:, 0:2 * KV],
                                  wkv_s[:, k, HI, :].bitcast(F32), ALU.subtract).then_inc(wkv_ready, 1)
            dve.wait_ge(const_loaded, 16 * N_CONST_DMA)

            def kv_block(n):
                for k in range(2):
                    c_split(n, k)
                kv_out(n - 1)
                for k in range(2, KC):
                    c_split(n, k)

            kv_block(1)
            with dve.Fori(2, N_BLK) as n:
                kv_block(n)

            def ln_stats(i, src):
                wait(dve, ln_rstd, i - 1)
                for h in range(2):
                    last = dve.bn_stats(st[:, h, :], src[:, h * 512:(h + 1) * 512])
                last.then_inc(ln_step, 1)

            def ln_settle(i):
                wait(dve, ln_step, i + 1)

            def ln_aggregate(par):
                dve.bn_aggr(mv[par][:, :], st[:, :, :].rearrange("p a b -> p (a b)")).then_inc(ln_var, 1)

            def ln_norm(i, par, src, dst, done):
                wait(dve, ln_rstd, i + 1)
                dve.tensor_scalar(dst, src, mv[par][:, 0:1], rstd[par][:, 0:1],
                                  ALU.subtract, ALU.mult).then_inc(done, 1)

            def x_stats(i):
                wait(dve, x_loaded[i % XRING], 16 * (i // XRING + 1))
                ln_stats(i, x_raw[i % XRING])
                ln_settle(i)
                ln_aggregate(i % 2)

            def x_norm(i):
                ln_norm(i, i % 2, x_raw[i % XRING][:, :], x_raw[i % XRING][:, :], xn_ready)

            def xt_out(i):
                n, t = i // TPB, i % TPB
                for r in range(2):
                    wait(dve, xt_hi, 2 * i + r + 1)
                    dst = act_of(n)
                    dve.tensor_tensor(dst[:, 4 * r:4 * r + 4, LO, t * P:(t + 1) * P],
                                      x_t[r][:, :].rearrange("p (k t) -> p k t", k=4),
                                      dst[:, 4 * r:4 * r + 4, HI, t * P:(t + 1) * P].bitcast(F32),
                                      ALU.subtract).then_inc(xt_ready, 1)

            for i in range(3):
                x_stats(i)
                x_norm(i)
            kv_out(N_BLK - 1)
            xt_out(0)
            x_stats(3)
            x_norm(3)
            for i in range(1, TPB):
                xt_out(i)
            x_stats(TPB)
            for n in range(N_BLK):
                for m in range(NKV):
                    i = TPB * (n + 1) + m // 2
                    if m % 2 == 0 and i < N_TILE:
                        x_norm(i)
                    if m % 2 == 1 and i + 1 < N_TILE:
                        x_stats(i + 1)
                    wait(dve, q_hi, NKV * n + m + 1)
                    dve.scalar_tensor_tensor(
                        out=proj[m % 2][:, :, LO, :], in0=bank[m % 4][:, :].rearrange("p (b t) -> p b t", b=TPB),
                        scalar=bq_s[:, m:m + 1], in1=proj[m % 2][:, :, HI, :].bitcast(F32),
                        op0=ALU.add, op1=ALU.subtract).then_inc(q_evac, 1)
                    if m % 2 == 0 and i < N_TILE:
                        xt_out(i)

            def row_max(b, u):
                wait(dve, qk_done, NKV * b + u + 1)
                dve.tensor_reduce(mx[u % 2][:, :], score[u % 2][:, :].rearrange("p (g k) -> p g k", g=G),
                                  AX, ALU.max).then_inc(max_done, 1)

            def neg_max(b, u):
                wait(dve, max_done, NKV * b + u + 1)
                dve.tensor_scalar(nb[u % 2][:, :], mx[u % 2][:, :], -SOFTMAX_SCALE, None,
                                  ALU.mult).then_inc(neg_max_ready, 1)

            def recip(b, u):
                wait(dve, exp_done, NKV * b + u + 1)
                dve.reciprocal(rsum[u % 2][:, :], sums[u % 2][:, :]).then_inc(rsum_ready, 1)

            def normalise(b, u):
                wait(dve, rsum_ready, NKV * b + u + 1)
                for g in range(G):
                    last = dve.tensor_scalar(pr[u % 2][:, g, :], pr[u % 2][:, g, :],
                                             rsum[u % 2][:, g:g + 1], None, ALU.mult)
                last.then_inc(prob_ready, 1)

            def y_out(b, half):
                wait(dve, y_hi, 2 * b + half + 1)
                dst = yt[:, 4 * half:4 * half + 4, :, :]
                dve.tensor_tensor(dst[:, :, LO, :], y_bank[:, :].rearrange("p (g q) -> p g q", g=G),
                                  dst[:, :, HI, :].bitcast(F32), ALU.subtract).then_inc(y_ready, 1)

            def x2_out(b, i, par, h):
                wait(dve, o_done, 2 * b + h + 1)
                wait(dve, xbo_ready, b + 1)
                wait(dve, out_stored[par], 16 * i)
                dve.tensor_tensor(x2[par][:, h * 512:(h + 1) * 512], bank[h][:, :],
                                  x_in[par][:, h * 512:(h + 1) * 512], ALU.add).then_inc(x2_ready, 1)

            def x2_stats(b, par):
                wait(dve, x2_ready, 2 * b + 2)
                ln_stats(N_TILE + b, x2[par])
                ln_settle(N_TILE + b)

            def x2_norm(b, par):
                wait(dve, x2t_done, 2 * b)
                ln_norm(N_TILE + b, par, x2[par][:, :], xn2[:, :], xn2_ready)

            def x2t_out(b, par, r):
                wait(dve, x2t_hi, 2 * b + r + 1)
                dve.scalar_tensor_tensor(
                    out=xnt[par][:, LO, 4 * r:4 * r + 4, :], in0=xt3[:, :].rearrange("p (k t) -> p k t", k=4),
                    scalar=FFN_UP, in1=xnt[par][:, HI, 4 * r:4 * r + 4, :],
                    op0=ALU.mult, op1=ALU.subtract).then_inc(x2t_ready, 1)

            def ffn_out(b, par, h):
                wait(dve, ffn_done, 2 * b + h + 1)
                cols = slice(h * 512, (h + 1) * 512)
                dve.scalar_tensor_tensor(out=x2[par][:, cols], in0=bank[0][:, :], scalar=scale_d[:, 0:1],
                                         in1=x2[par][:, cols], op0=ALU.mult, op1=ALU.add).then_inc(out_ready, 1)

            def unit(b, u, attn, prev):
                pb, pu = (b, u - 1) if u else (b - 1, NKV - 1)
                if attn:
                    row_max(b, u)
                    neg_max(b, u)
                if prev:
                    recip(pb, pu)
                    normalise(pb, pu)

            def step(b, i, par, attn, tail1, tail2):
                for u in range(NKV):
                    unit(b, u, attn, tail1 if u == 0 else attn)
                    if u == 0:
                        if tail2:
                            x2t_out(b - 2, par, 1)
                        if tail1:
                            y_out(b - 1, 1)
                        if tail2:
                            ffn_out(b - 2, par, 0)
                    if u == 3 and tail1:
                        x2_out(b - 1, i - 1 + par, 1 - par, 0)
                    if u == 5:
                        if tail1:
                            x2_out(b - 1, i - 1 + par, 1 - par, 1)
                            x2_stats(b - 1, 1 - par)
                        if attn:
                            y_out(b, 0)
                        if tail1:
                            ln_aggregate(1 - par)
                    if u == 6 and tail1:
                        x2_norm(b - 1, 1 - par)
                    if u == 7:
                        if tail1:
                            x2t_out(b - 1, 1 - par, 0)
                        if tail2:
                            ffn_out(b - 2, par, 1)

            dve.wait_ge(const_made, 7)
            step(0, 0, 0, True, False, False)
            step(1, 0, 1, True, True, False)
            step(2, 1, 0, True, True, True)
            step(3, 1, 1, True, True, True)
            with dve.Fori(2, N_BATCH // 2) as i:
                step(2 * i, i, 0, True, True, True)
                step(2 * i + 1, i, 1, True, True, True)
            step(N_BATCH, N_BATCH // 2, 0, False, True, True)
            step(N_BATCH + 1, N_BATCH // 2, 1, False, False, True)

        @block.tensor
        def _(pe):
            def kv_chunk(n, k, first_block):
                wait(pe, c_ready, KC * n + k + 1)
                if first_block:
                    wait(pe, wkv_ready, k + 1)
                a = act[0]
                for g in range(6):
                    if k == 0:
                        wait(pe, kv_evac, 6 * (n - 1) + g + 1)
                    for p, (w_part, a_part) in enumerate(((HI, HI), (HI, LO), (LO, HI))):
                        start, stop = k == 0 and p == 0, k == KC - 1 and p == 2
                        if g < 2:
                            last = pe.matmul(bank[g][:, :], wkv_s[:, k, w_part, g * P:(g + 1) * P],
                                             a[:, k, a_part, :], start=start, stop=stop)
                        else:
                            last = pe.matmul(bank[g][:, 0:KV], a[:, k, w_part, (g - 2) * P:(g - 1) * P],
                                             wkv_s[:, k, a_part, KV:2 * KV], start=start, stop=stop)
                    if k == KC - 1:
                        last.then_inc(kv_done, 1)
                if k < KC - 1:
                    last.then_inc(c_used, 1)

            for k in range(KC):
                kv_chunk(0, k, True)
            with pe.Fori(1, N_BLK) as n:
                for k in range(KC):
                    kv_chunk(n, k, False)

            def transpose_x(i):
                wait(pe, xn_ready, i + 1)
                for r in range(2):
                    wait(pe, xt_ready, 2 * (i - 1) + r + 1)
                    for k in range(4):
                        c = 4 * r + k
                        last = pe.transpose(x_t[r][:, k * P:(k + 1) * P],
                                            x_raw[i % XRING][:, c * P:(c + 1) * P], ident[:, :])
                    last.then_inc(xt_done, 1)

            pe.wait_ge(const_made, 6)
            for i in range(TPB):
                transpose_x(i)
            pe.wait_ge(wq_ready, KC)
            pe.wait_ge(kv_evac, 6 * N_BLK)
            for n in range(N_BLK):
                wait(pe, xt_ready, 2 * TPB * (n + 1))
                a = act_of(n)
                for m in range(NKV):
                    wait(pe, q_evac, NKV * n + m - 3)
                    for k in range(KC):
                        for p, (w_part, a_part) in enumerate(((HI, HI), (HI, LO), (LO, HI))):
                            last = pe.matmul(bank[m % 4][:, :], wq_s[:, k, w_part, m * P:(m + 1) * P],
                                             a[:, k, a_part, :], start=k == 0 and p == 0,
                                             stop=k == KC - 1 and p == 2)
                    last.then_inc(q_done, 1)
                    if m % 2 == 0 and n < N_BLK - 1:
                        transpose_x(TPB * (n + 1) + m // 2)

            def scores(b, i, par, u):
                if u == 0:
                    wait(pe, qv_loaded[par], 32 * (i + 1))
                if u % 4 == 0:
                    wait(pe, kd_loaded[u // 4], 4 * 16 * (b + 1))
                wait(pe, exp_done, NKV * b + u - 1)
                for p, (q_part, k_part) in enumerate(((HI, HI), (HI, LO), (LO, HI))):
                    last = pe.matmul(score[u % 2][:, :], q_s[par][:, u, q_part, :], kd[:, u, k_part, :],
                                     start=p == 0, stop=p == 2)
                last.then_inc(qk_done, 1)

            def transpose_p(b, u):
                wait(pe, prob_ready, NKV * b + u + 1)
                wait(pe, pt_ready, NKV * b + u - 1)
                for g in range(G):
                    last = pe.transpose(prob_t[u % 2][:, g * P:(g + 1) * P], pr[u % 2][:, g, :], ident[:, :])
                last.then_inc(tp_done, 1)

            def attend(b, par, half):
                wait(pe, pt_ready, NKV * b + 4 * half + 4)
                wait(pe, y_ready, 2 * b + half)
                for c in range(4):
                    u = 4 * half + c
                    last = pe.matmul(y_bank[c * HD:(c + 1) * HD, :], v_s[par][:, u * HD:(u + 1) * HD],
                                     pt[:, u, :], start=True, stop=True)
                last.then_inc(pv_done, 1)

            def project(b, quarter):
                h, k0 = quarter // 2, 4 * (quarter % 2)
                if quarter == 0:
                    wait(pe, y_ready, 2 * b + 2)
                    wait(pe, out_ready, 2 * (b - 1) + 1)
                if quarter == 2:
                    wait(pe, x2_ready, 2 * b)
                for k in range(k0, k0 + 4):
                    for p, (y_part, w_part) in enumerate(((HI, HI), (HI, LO), (LO, HI))):
                        last = pe.matmul(bank[h][:, :], yt[:, k, y_part, :],
                                         wo_chunk(k, w_part)[:, h * 512:(h + 1) * 512],
                                         start=k == 0 and p == 0, stop=k == KC - 1 and p == 2)
                if quarter % 2:
                    last.then_inc(o_done, 1)

            def transpose_x2(b, r):
                wait(pe, xn2_ready, b + 1)
                wait(pe, x2t_ready, 2 * b + r)
                for k in range(4):
                    c = 4 * r + k
                    last = pe.transpose(xt3[:, k * P:(k + 1) * P], xn2[:, c * P:(c + 1) * P], ident[:, :])
                last.then_inc(x2t_done, 1)

            def ffn(b, par, h, k0, k1):
                if k0 == 0:
                    wait(pe, x2t_ready, 2 * b + 2)
                    if h == 0:
                        wait(pe, out_ready, 2 * b)
                    else:
                        wait(pe, out_ready, 2 * b + 1)
                for k in range(k0, k1):
                    for part in (HI, LO):
                        last = pe.matmul(bank[0][:, :], xnt[par][:, part, k, :],
                                         ffn_s[:, k, h * 512:(h + 1) * 512],
                                         start=k == 0 and part == HI, stop=k == KC - 1 and part == LO)
                if k1 == KC:
                    last.then_inc(ffn_done, 1)

            def step(b, i, par, attn, tail1, tail2):
                for u in range(NKV):
                    if attn:
                        scores(b, i, par, u)
                    if u == 0:
                        if tail2:
                            transpose_x2(b - 2, 1)
                        if tail1:
                            transpose_p(b - 1, 7)
                            attend(b - 1, 1 - par, 1)
                        if tail2:
                            ffn(b - 2, par, 0, 0, KC)
                    if 1 <= u <= 4 and tail1:
                        project(b - 1, u - 1)
                    if u in (5, 6) and tail2:
                        if u == 5 and tail1:
                            wait(pe, x2_ready, 2 * b - 1)
                        ffn(b - 2, par, 1, 4 * (u - 5), 4 * (u - 4))
                    if u and attn:
                        transpose_p(b, u - 1)
                    if u == 5 and attn:
                        attend(b, par, 0)
                    if u == 7 and tail1:
                        transpose_x2(b - 1, 0)

            step(0, 0, 0, True, False, False)
            pe.wait_ge(wo_ready, KC)
            step(1, 0, 1, True, True, False)
            pe.wait_ge(ffn_ready, KC)
            step(2, 1, 0, True, True, True)
            step(3, 1, 1, True, True, True)
            with pe.Fori(2, N_BATCH // 2) as i:
                step(2 * i, i, 0, True, True, True)
                step(2 * i + 1, i, 1, True, True, True)
            step(N_BATCH, N_BATCH // 2, 0, False, True, True)
            step(N_BATCH + 1, N_BATCH // 2, 1, False, False, True)


def kernel(x, ctx_4096, L0_xattn_Wq, L0_xattn_bq, L0_xattn_Wk, L0_xattn_bk, L0_xattn_Wv, L0_xattn_bv,
           L0_xattn_Wo, L0_xattn_bo, L0_ffn_kernel, L0_ffn_scale):
    import numpy as np
    import concourse.bacc as bacc
    from concourse.bass_utils import run_bass_kernel_spmd

    wo_rows = np.asarray(L0_xattn_Wo).reshape(2, 4, G, HD, D).transpose(0, 2, 1, 3, 4).reshape(D, D)
    arrays = {
        "x": np.asarray(x).reshape(N_BATCH * P, D),
        "ctx_t": np.asarray(ctx_4096).reshape(N_BATCH * P, D).T,
        "wq": np.asarray(L0_xattn_Wq),
        "bq": np.asarray(L0_xattn_bq).reshape(KC, P).T,
        "wkv": np.concatenate([np.asarray(L0_xattn_Wk), np.asarray(L0_xattn_Wv)], axis=1),
        "bk": np.asarray(L0_xattn_bk).reshape(2, P).T,
        "bv": np.asarray(L0_xattn_bv),
        "wo": wo_rows,
        "bo": np.asarray(L0_xattn_bo),
        "ffn_w": np.asarray(L0_ffn_kernel),
        "ffn_scale": np.asarray(L0_ffn_scale).reshape(1),
    }
    arrays = {n: np.ascontiguousarray(a) for n, a in arrays.items()}
    nc = bacc.Bacc("TRN2", target_bir_lowering=False, num_devices=1)
    args = [nc.dram_tensor(n, a.shape, mybir.dt.from_np(a.dtype), kind="ExternalInput").ap()
            for n, a in arrays.items()]
    out = nc.dram_tensor("out", (N_BATCH * P, D), F32, kind="ExternalOutput").ap()
    attention_ffn(nc, *args, out)
    r = run_bass_kernel_spmd(nc, [arrays], core_ids=[0])
    return np.asarray(r.results[0]["out"]).reshape(N_BATCH, P, D)
```

```python
import concourse.bass as bass
from concourse import mybir

F32 = mybir.dt.float32
F32R = mybir.dt.float32r
F16 = mybir.dt.float16
U8 = mybir.dt.uint8
ALU = mybir.AluOpType
ACT = mybir.ActivationFunctionType
AX = mybir.AxisListType.X

P = 128
N_BATCH = 16
D = 1024
KC = D // P
BLK = 512
N_BLK = N_BATCH * P // BLK
TPB = BLK // P
HD = 32
NKV = 8
G = 4
KV = NKV * HD
HI, LO = 0, 1
EPS = 1e-5
SOFTMAX_SCALE = float(HD) ** -0.5
P_EXC = 0.8
N_EXC = round(D * P_EXC)
INHIBIT = -4.0
FFN_UP = 256.0
WRING = 3
CRING = 4
XRING = 4
KB = 1024


def wait(engine, semaphore, count):
    if isinstance(count, int) and count <= 0:
        return
    engine.wait_ge(semaphore, count)


def attention_ffn(nc, x, ctx_t, wq, bq, wkv, bk, bv, wo, bo, ffn_w, ffn_scale, out):
    base = (nc.sbuf_base + 31) // 32 * 32
    R_KV = base
    R_Q = R_KV + 32 * KB
    R_A1 = R_Q + 64 * KB
    R_A0 = R_A1 + 32 * KB
    R_W = R_A0 + 32 * KB
    R_C = R_W + WRING * 4 * KB
    R_O = R_C + CRING * 2 * KB
    R_S = R_O + 8 * KB
    R_END = R_S + 9 * KB

    def at(name, shape, dtype, offset):
        return nc.alloc_sbuf_tensor_at(name, shape, dtype, offset=offset)

    cursor = [R_END]

    def const(name, shape, dtype):
        size = 4
        for s in shape[1:]:
            size *= s
        t = at(name, shape, dtype, cursor[0])
        cursor[0] += (size + 31) // 32 * 32
        return t

    wkv_s = at("wkv_s", [P, KC, 2, 2 * KV], F32R, R_KV)
    wq_s = at("wq_s", [P, NKV, KC, 2, P], F32R, R_Q)
    act = [at(f"act{i}", [P, KC, 2, BLK], F32R, r) for i, r in ((0, R_A0), (1, R_A1))]
    w_raw = [at(f"w_raw{i}", [P, D], F32, R_W + i * 4 * KB) for i in range(WRING)]
    c_raw = [at(f"c_raw{i}", [P, BLK], F32, R_C + i * 2 * KB) for i in range(CRING)]
    x_raw = [at(f"x_raw{i}", [P, D], F32, R_W + i * 4 * KB if i < WRING else R_S + 4 * KB)
             for i in range(XRING)]
    proj = [at(f"proj{i}", [P, TPB, 2, P], F32R, R_O + i * 4 * KB) for i in range(2)]
    v_out = at("v_out", [P, TPB, KV], F32, R_S)
    wo_lo4 = at("wo_lo4", [P, KC // 2, 2, D], F32R, R_KV)
    wo_hi4 = at("wo_hi4", [P, KC // 2, 2, D], F32R, R_Q)
    ffn_s = at("ffn_s", [P, KC, D], F16, R_Q + 32 * KB)
    x_in = [at(f"x_in{i}", [P, D], F32, R_Q + (48 + 4 * i) * KB) for i in range(2)]
    x2 = [at(f"x2_{i}", [P, D], F32, R_Q + (56 + 4 * i) * KB) for i in range(2)]
    kd = at("kd", [P, NKV, 2, 2 * P], F32R, R_A1)
    ffn_raw = at("ffn_raw", [P, KC, D], U8, R_A1 + 16 * KB)
    wo_raw = [at(f"wo_raw{i}", [P, D], F32, r) for i, r in enumerate(
        (R_C, R_C + 4 * KB, R_A1 + 16 * KB, R_A1 + 20 * KB))]
    yt = at("yt", [P, KC, 2, P], F32R, R_A0)
    xn2 = at("xn2", [P, D], F32, R_A0 + 8 * KB)
    xnt = [at(f"xnt{i}", [P, 2, KC, P], F16, R_A0 + (12 + 4 * i) * KB) for i in range(2)]
    pr = [at(f"pr{i}", [P, G, P], F32, R_W + i * 2 * KB) for i in range(2)]
    pt = at("pt", [P, NKV, G * P], F32, R_W + 4 * KB)
    q_s = [at("q_s0", [P, NKV, 2, P], F32R, R_S), at("q_s1", [P, NKV, 2, P], F32R, R_A1 + 24 * KB)]
    v_s = [at("v_s0", [P, KV], F32, R_S + 8 * KB), const("v_s1", [P, KV], F32)]
    ident = const("ident", [P, P], F32)
    ffn_sign = const("ffn_sign", [P, KC], F32)
    bq_s = const("bq_s", [P, KC], F32)
    bk_s = const("bk_s", [P, 2], F32)
    bv_s = const("bv_s", [P, KV], F32)
    bo_s = const("bo_s", [P, D], F32)
    scale_s = const("scale_s", [P, 1], F32)
    scale_d = const("scale_d", [P, 1], F32)
    minus_half = const("minus_half", [P, 1], F32)
    eps_s = const("eps_s", [P, 1], F32)
    st = const("st", [P, 2, 6], F32)
    mv = [const(f"mv{i}", [P, 2], F32) for i in range(2)]
    ve = const("ve", [P, 1], F32)
    rstd = [const(f"rstd{i}", [P, 1], F32) for i in range(2)]
    mx = [const(f"mx{i}", [P, G], F32) for i in range(2)]
    nb = [const(f"nb{i}", [P, G], F32) for i in range(2)]
    sums = [const(f"sums{i}", [P, G], F32) for i in range(2)]
    rsum = [const(f"rsum{i}", [P, G], F32) for i in range(2)]
    assert cursor[0] <= nc.sbuf_usable_end, (cursor[0], nc.sbuf_usable_end)

    bank = [nc.alloc_psum_tensor(f"bank{i}", [P, 512], F32) for i in range(8)]
    score, prob_t, x_t = bank[4:6], bank[6:8], bank[6:8]
    y_bank = bank[2]
    o_bank = [bank[0], bank[1]]
    x2t_bank = [bank[0], bank[2]]
    ffn_bank = [bank[3], bank[1]]

    q_d = nc.dram_tensor("q_d", [N_BATCH, P, NKV, 2, P], F32)
    k_d = nc.dram_tensor("k_d", [N_BATCH, HD, NKV, 2, P], F32)
    v_d = nc.dram_tensor("v_d", [N_BATCH, P, KV], F32)

    S = {n: nc.alloc_semaphore(n) for n in (
        "const_loaded", "const_made", "c_loaded0", "c_loaded1", "c_loaded2", "c_loaded3",
        "wkv_loaded0", "wkv_loaded1", "wkv_loaded2",
        "wkv_hi", "wkv_ready", "c_hi", "c_ready", "c_used", "kv_done", "k_hi", "kv_evac",
        "k_stored", "v_stored", "wq_loaded0", "wq_loaded1", "wq_loaded2", "wq_hi", "wq_ready",
        "x_loaded0", "x_loaded1", "x_loaded2", "x_loaded3", "ln_step", "ln_var", "ln_ve",
        "ln_rstd", "xn_ready", "xt_done", "xt_hi", "xt_ready", "q_done", "q_hi", "q_evac",
        "q_stored0", "q_stored1", "wo_loaded0", "wo_loaded1", "wo_hi", "wo_ready",
        "ffn_loaded", "ffn_ready", "kd_zeroed",
        "kd_loaded0", "kd_loaded1", "qv_loaded0", "qv_loaded1", "x_in_loaded0", "x_in_loaded1",
        "qk_done", "max_done", "neg_max_ready", "exp_done", "rsum_ready", "prob_ready", "tp_done",
        "pt_ready", "pv_done", "y_hi", "y_ready", "xbo_ready", "o_done", "x2_ready",
        "xn2_ready", "x2t_done", "x2t_hi", "x2t_ready", "ffn_done", "out_ready",
        "out_stored0", "out_stored1")}
    (const_loaded, const_made, wkv_hi, wkv_ready, c_hi, c_ready, c_used, kv_done, k_hi, kv_evac,
     k_stored, v_stored, wq_hi, wq_ready, ln_step, ln_var, ln_ve, ln_rstd, xn_ready, xt_done,
     xt_hi, xt_ready, q_done, q_hi, q_evac, wo_hi, wo_ready, ffn_loaded, ffn_ready, kd_zeroed,
     qk_done, max_done, neg_max_ready, exp_done, rsum_ready, prob_ready, tp_done, pt_ready,
     pv_done, y_hi, y_ready, xbo_ready, o_done, x2_ready, xn2_ready, x2t_done, x2t_hi,
     x2t_ready, ffn_done, out_ready) = (S[n] for n in (
         "const_loaded", "const_made", "wkv_hi", "wkv_ready", "c_hi", "c_ready", "c_used",
         "kv_done", "k_hi", "kv_evac", "k_stored", "v_stored", "wq_hi", "wq_ready", "ln_step",
         "ln_var", "ln_ve", "ln_rstd", "xn_ready", "xt_done", "xt_hi", "xt_ready", "q_done",
         "q_hi", "q_evac", "wo_hi", "wo_ready", "ffn_loaded", "ffn_ready", "kd_zeroed",
         "qk_done", "max_done", "neg_max_ready", "exp_done", "rsum_ready", "prob_ready",
         "tp_done", "pt_ready", "pv_done", "y_hi", "y_ready", "xbo_ready", "o_done", "x2_ready",
         "xn2_ready", "x2t_done", "x2t_hi", "x2t_ready", "ffn_done", "out_ready"))
    c_loaded = [S[f"c_loaded{i}"] for i in range(CRING)]
    wkv_loaded = [S[f"wkv_loaded{i}"] for i in range(WRING)]
    wq_loaded = [S[f"wq_loaded{i}"] for i in range(WRING)]
    x_loaded = [S[f"x_loaded{i}"] for i in range(XRING)]
    wo_loaded = [S["wo_loaded0"], S["wo_loaded1"]]
    q_stored = [S["q_stored0"], S["q_stored1"]]
    kd_loaded = [S["kd_loaded0"], S["kd_loaded1"]]
    qv_loaded = [S["qv_loaded0"], S["qv_loaded1"]]
    x_in_loaded = [S["x_in_loaded0"], S["x_in_loaded1"]]
    out_stored = [S["out_stored0"], S["out_stored1"]]

    N_CONST_DMA = 5
    N_TILE = N_BATCH
    block = nc.Block()

    def wo_chunk(kk, part):
        half = wo_lo4 if kk < KC // 2 else wo_hi4
        return half[:, kk % (KC // 2), part, :]

    def act_of(n):
        return act[(n + 1) % 2]

    with block:

        @block.sync
        def _(sp):
            def load_c(n, k):
                wait(sp, c_ready, KC * n + k + 1 - CRING)
                sp.dma_start(c_raw[k % CRING][:, :],
                             ctx_t[k * P:(k + 1) * P, bass.ds(n * BLK, BLK)]).then_inc(c_loaded[k % CRING], 16)

            def store_kv(n):
                for j in range(2):
                    wait(sp, kv_evac, 6 * n + j + 1)
                    for c in range(4):
                        sp.dma_start(
                            k_d[bass.ds(n * TPB, TPB), :, 4 * j + c, :, :].rearrange("b d h t -> d b (h t)"),
                            proj[j][c * HD:(c + 1) * HD, :, :, :].rearrange("d b h t -> d b (h t)").bitcast(F32),
                        ).then_inc(k_stored, 16)
                wait(sp, kv_evac, 6 * n + 6)
                sp.dma_start(v_d[bass.ds(n * TPB, TPB), :, :].rearrange("b p v -> p b v"),
                             v_out[:, :, :]).then_inc(v_stored, 16)

            for k in range(KC):
                load_c(0, k)
                wait(sp, wkv_ready, k + 1 - WRING)
                sp.dma_start(w_raw[k % WRING][:, 0:2 * KV],
                             wkv[k * P:(k + 1) * P, :]).then_inc(wkv_loaded[k % WRING], 16)
                if k == 1:
                    sp.dma_start(bq_s[:, :], bq).then_inc(const_loaded, 16)
                    sp.dma_start(bk_s[:, :], bk).then_inc(const_loaded, 16)
                    sp.dma_start(bv_s[:, :], bv.partition_broadcast(P)).then_inc(const_loaded, 16)
                    sp.dma_start(bo_s[:, :], bo.partition_broadcast(P)).then_inc(const_loaded, 16)
                    sp.dma_start(scale_s[:, :], ffn_scale.partition_broadcast(P)).then_inc(const_loaded, 16)
            with sp.Fori(1, N_BLK - 1) as n:
                for k in range(KC):
                    load_c(n, k)
                store_kv(n - 1)

            def load_x(i):
                wait(sp, xt_done, 2 * (i - XRING + 1))
                sp.dma_start(x_raw[i % XRING][:, :],
                             x[i * P:(i + 1) * P, :]).then_inc(x_loaded[i % XRING], 16)

            wait(sp, wq_ready, KC)
            for k in range(KC):
                if k % 2 == 0:
                    load_x(k // 2)
                load_c(N_BLK - 1, k)
            store_kv(N_BLK - 2)
            for i in range(XRING, 2 * XRING):
                load_x(i)
            store_kv(N_BLK - 1)

            def store_q(n, m):
                wait(sp, q_evac, NKV * n + m + 1)
                sp.dma_start(
                    q_d[n * TPB:(n + 1) * TPB, :, m, :, :].rearrange("b p h t -> p b (h t)"),
                    proj[m % 2][:, :, :, :].rearrange("p b h t -> p b (h t)").bitcast(F32),
                ).then_inc(q_stored[m % 2], 16)

            def load_kd(b, half):
                for e in range(2):
                    for part in range(2):
                        row = (2 * e + part) * HD
                        sp.dma_start(
                            kd[row:row + HD, 4 * half:4 * half + 4, :, e * P:(e + 1) * P]
                            .rearrange("p c h t -> p (c h) t").bitcast(F32),
                            k_d[b, :, 4 * half:4 * half + 4, :, :].rearrange("d c h t -> d (c h) t"),
                        ).then_inc(kd_loaded[half], 16)

            def load_qv(b, par):
                for e in range(2):
                    for part in range(2):
                        row = (2 * e + part) * HD
                        for pair in range(2):
                            g = 2 * pair + e
                            sp.dma_start(q_s[par][row:row + HD, :, pair, :].bitcast(F32),
                                         q_d[b, g * HD:(g + 1) * HD, :, part, :]).then_inc(qv_loaded[par], 16)
                sp.dma_start(v_s[par][:, :], v_d[b]).then_inc(qv_loaded[par], 16)

            def load_x_in(b, par):
                sp.dma_start(x_in[par][:, :], x[bass.ds(b * P, P), :]).then_inc(x_in_loaded[par], 16)

            for n in range(N_BLK):
                for m in range(NKV):
                    store_q(n, m)
                    if m % 2 == 0 and n < N_BLK - 2:
                        load_x(4 * (n + 2) + m // 2)
                    if n == N_BLK - 1 and m == 1:
                        wait(sp, k_stored, 8 * 16 * N_BLK)
                        wait(sp, q_stored[0], 16 * 4)
                        wait(sp, q_stored[1], 16 * 4)
                        wait(sp, v_stored, 16 * N_BLK)
                        wait(sp, xt_done, 2 * N_TILE)
                        wait(sp, kd_zeroed, 1)
                        load_kd(0, 0)
                        load_qv(0, 0)
                        load_kd(0, 1)
                        load_qv(1, 1)
                    if n == N_BLK - 1 and m == 5:
                        wait(sp, qk_done, 4)
                        load_kd(1, 0)
                    if n == N_BLK - 1 and m == 6:
                        load_x_in(0, 0)
            wait(sp, qk_done, NKV)
            load_kd(1, 1)
            wait(sp, q_stored[0], 16 * 4 * N_BLK)
            wait(sp, q_stored[1], 16 * 4 * N_BLK)

            def step(b, i, par, attn, more, t3):
                if attn:
                    wait(sp, x2_ready, 2 * (b - 2) + 2)
                    load_x_in(b, par)
                if t3:
                    wait(sp, out_ready, 2 * (b - 3) + 2)
                    sp.dma_start(out[bass.ds((b - 3) * P, P), :], x2[1 - par][:, :]).then_inc(out_stored[1 - par], 16)
                if more:
                    wait(sp, pv_done, 2 * b)
                    load_qv(b + 1, 1 - par)
                    wait(sp, qk_done, NKV * b + 4)
                    load_kd(b + 1, 0)
                    wait(sp, qk_done, NKV * b + 8)
                    load_kd(b + 1, 1)

            step(1, 0, 1, True, True, False)
            step(2, 1, 0, True, True, False)
            step(3, 1, 1, True, True, True)
            last = N_BATCH // 2 - 1
            with sp.Fori(2, last) as i:
                step(2 * i, i, 0, True, True, True)
                step(2 * i + 1, i, 1, True, True, True)
            step(2 * last, last, 0, True, True, True)
            step(2 * last + 1, last, 1, True, False, True)
            step(N_BATCH, last + 1, 0, False, False, True)
            step(N_BATCH + 1, last + 1, 1, False, False, True)
            step(N_BATCH + 2, last + 2, 0, False, False, True)
            wait(sp, out_stored[0], 16 * N_BATCH // 2)
            wait(sp, out_stored[1], 16 * N_BATCH // 2)

        @block.gpsimd
        def _(pool):
            pool.memset(ident[:, :], 0.0).then_inc(const_made, 1)
            pool.memset(ffn_sign[:, :], 1.0).then_inc(const_made, 1)
            pool.memset(minus_half[:, :], -0.5).then_inc(const_made, 1)
            pool.memset(eps_s[:, :], EPS).then_inc(const_made, 1)
            pool.wait_ge(const_made, 4)
            pool.affine_select(out=ident[:, :], in_=ident[:, :], compare_op=ALU.not_equal, fill=1.0,
                               base=0, pattern=[[-1, P]], channel_multiplier=1).then_inc(const_made, 1)
            pool.affine_select(out=ffn_sign[:, :], in_=ffn_sign[:, :], compare_op=ALU.is_ge, fill=INHIBIT,
                               base=N_EXC - 1, pattern=[[-P, KC]], channel_multiplier=-1).then_inc(const_made, 1)
            pool.wait_ge(const_made, 6)
            pool.wait_ge(const_loaded, 16 * N_CONST_DMA)
            pool.tensor_scalar(scale_d[:, :], scale_s[:, :], 1.0 / FFN_UP, None, ALU.mult).then_inc(const_made, 1)

            def load_wq(k):
                if k < WRING:
                    pool.wait_ge(wkv_ready, KC)
                else:
                    pool.wait_ge(wq_ready, k - WRING + 1)
                pool.dma_start(w_raw[k % WRING][:, :], wq[k * P:(k + 1) * P, :]).then_inc(wq_loaded[k % WRING], 16)

            for k in range(WRING - 1):
                load_wq(k)
            for k in range(KC):
                if k + WRING - 1 < KC:
                    load_wq(k + WRING - 1)
                raw = w_raw[k % WRING][:, :].rearrange("p (m c) -> p m c", m=NKV)
                pool.wait_ge(wq_hi, k + 1)
                pool.tensor_tensor(wq_s[:, :, k, LO, :], raw, wq_s[:, :, k, HI, :].bitcast(F32),
                                   ALU.subtract).then_inc(wq_ready, 1)

            def inv_std(i, par):
                wait(pool, ln_var, i + 1)
                pool.tensor_tensor(ve[:, :], mv[par][:, 1:2], eps_s[:, :], ALU.add).then_inc(ln_ve, 1)
                wait(pool, ln_ve, i + 1)
                pool.tensor_tensor(rstd[par][:, :], ve[:, :], minus_half[:, :], ALU.pow).then_inc(ln_rstd, 1)

            def wo_slot(k):
                return wo_raw[k % 2 + 2 * (k // 4)]

            def load_wo(k):
                if k == 0:
                    pool.wait_ge(c_ready, KC * N_BLK)
                if k == 4:
                    pool.wait_ge(q_done, NKV * (N_BLK - 1))
                if k % 4 >= 2:
                    pool.wait_ge(wo_ready, k - 1)
                pool.dma_start(wo_slot(k)[:, :], wo[k * P:(k + 1) * P, :]).then_inc(wo_loaded[k % 2], 16)

            def split_wo(k):
                pool.wait_ge(wo_loaded[k % 2], 16 * (k // 2 + 1))
                if k == 0:
                    pool.wait_ge(kv_done, 6 * N_BLK)
                if k >= KC // 2:
                    pool.wait_ge(q_done, NKV * (N_BLK - 1) + k - 3)
                pool.tensor_copy(wo_chunk(k, HI), wo_slot(k)[:, :]).then_inc(wo_hi, 1)
                pool.wait_ge(wo_hi, k + 1)
                pool.tensor_tensor(wo_chunk(k, LO), wo_slot(k)[:, :], wo_chunk(k, HI).bitcast(F32),
                                   ALU.subtract).then_inc(wo_ready, 1)
                if k % 4 < 2:
                    load_wo(k + 2)

            for i in range(5):
                inv_std(i, i % 2)
            load_wo(0)
            load_wo(1)
            for i in range(5, N_TILE):
                if i - 5 < KC // 2:
                    split_wo(i - 5)
                inv_std(i, i % 2)
            pool.wait_ge(q_done, NKV * (N_BLK - 1))
            pool.memset(kd[:, :, :, :].rearrange("p a b c -> p (a b c)").bitcast(F32), 0.0).then_inc(kd_zeroed, 1)

            def add_bo(b, i, par):
                wait(pool, x_in_loaded[par], 16 * (i + 1))
                pool.tensor_tensor(x_in[par][:, :], x_in[par][:, :], bo_s[:, :], ALU.add).then_inc(xbo_ready, 1)

            load_wo(4)
            load_wo(5)
            for k in range(KC // 2, KC):
                split_wo(k)
            pool.wait_ge(wo_ready, KC)
            pool.dma_start(ffn_raw[:, :, :], ffn_w.rearrange("(k p) n -> p k n", p=P)).then_inc(ffn_loaded, 16)
            add_bo(0, 0, 0)
            add_bo(1, 0, 1)
            inv_std(N_TILE, 0)
            add_bo(2, 1, 0)
            inv_std(N_TILE + 1, 1)
            add_bo(3, 1, 1)
            inv_std(N_TILE + 2, 0)
            with pool.Fori(2, N_BATCH // 2) as i:
                add_bo(2 * i, i, 0)
                inv_std(N_TILE + 2 * i - 1, 1)
                add_bo(2 * i + 1, i, 1)
                inv_std(N_TILE + 2 * i, 0)
            inv_std(N_TILE + N_BATCH - 1, 1)

        @block.scalar
        def _(sc):
            def c_split(n, k):
                wait(sc, c_loaded[k % CRING], 16 * (2 * n + k // CRING + 1))
                if k < KC - 1:
                    wait(sc, c_used, (KC - 1) * (n - 1) + k + 1)
                else:
                    wait(sc, kv_done, 6 * n)
                sc.activation(act[0][:, k, HI, :], c_raw[k % CRING][:, :], ACT.Copy).then_inc(c_hi, 1)

            def k_evac(n):
                for j in range(2):
                    wait(sc, kv_done, 6 * n + j + 1)
                    wait(sc, k_stored, 8 * 16 * n)
                    sc.activation(proj[j][:, :, HI, :], bank[j][:, :].rearrange("p (b t) -> p b t", b=TPB),
                                  ACT.Identity, bias=bk_s[:, j:j + 1]).then_inc(k_hi, 1)

            for k in range(KC):
                c_split(0, k)
                sc.wait_ge(wkv_loaded[k % WRING], 16 * (k // WRING + 1))
                sc.activation(wkv_s[:, k, HI, :], w_raw[k % WRING][:, 0:2 * KV], ACT.Copy).then_inc(wkv_hi, 1)
            sc.wait_ge(const_loaded, 16 * N_CONST_DMA)

            def wq_split(k):
                sc.wait_ge(wq_loaded[k % WRING], 16 * (k // WRING + 1))
                sc.activation(wq_s[:, :, k, HI, :], w_raw[k % WRING][:, :].rearrange("p (m c) -> p m c", m=NKV),
                              ACT.Copy).then_inc(wq_hi, 1)

            def kv_block(n, with_wq=False):
                for k in range(KC):
                    c_split(n, k)
                    if k == 1:
                        k_evac(n - 1)
                    if with_wq:
                        wq_split(k)

            kv_block(1, with_wq=True)
            with sc.Fori(2, N_BLK - 1) as n:
                kv_block(n)

            def xt_evac(i):
                n, t = i // TPB, i % TPB
                for r in range(2):
                    wait(sc, xt_done, 2 * i + r + 1)
                    wait(sc, q_done, NKV * (n - 1))
                    sc.activation(act_of(n)[:, 4 * r:4 * r + 4, HI, t * P:(t + 1) * P],
                                  x_t[r][:, :].rearrange("p (k t) -> p k t", k=4), ACT.Copy).then_inc(xt_hi, 1)

            for k in range(KC):
                c_split(N_BLK - 1, k)
                if k == 1:
                    k_evac(N_BLK - 2)
            for i in range(TPB):
                xt_evac(i)
            k_evac(N_BLK - 1)

            def q_out(n, m):
                wait(sc, q_done, NKV * n + m + 1)
                if n == 0:
                    wait(sc, k_stored, 8 * 16 * N_BLK)
                wait(sc, q_stored[m % 2], 16 * (4 * n + m // 2))
                sc.activation(proj[m % 2][:, :, HI, :], bank[m % 4][:, :].rearrange("p (b t) -> p b t", b=TPB),
                              ACT.Identity, bias=bq_s[:, m:m + 1]).then_inc(q_hi, 1)

            for n in range(N_BLK - 1):
                for m in range(NKV):
                    q_out(n, m)
                    if m % 2 == 0:
                        xt_evac(TPB * (n + 1) + m // 2)

            def exps(b, u):
                par = u % 2
                wait(sc, neg_max_ready, NKV * b + u + 1)
                wait(sc, tp_done, NKV * b + u - 1)
                for g in range(G):
                    last = sc.activation(pr[par][:, g, :], score[par][:, g * P:(g + 1) * P], ACT.Exp,
                                         bias=nb[par][:, g:g + 1], scale=SOFTMAX_SCALE,
                                         accum_out=sums[par][:, g:g + 1])
                last.then_inc(exp_done, 1)

            def pt_evac(b, u):
                wait(sc, tp_done, NKV * b + u + 1)
                wait(sc, pv_done, 2 * (b - 1) + u // 4 + 1)
                sc.activation(pt[:, u, :], prob_t[u % 2][:, :], ACT.Copy).then_inc(pt_ready, 1)

            def y_evac(b, half):
                wait(sc, pv_done, 2 * b + half + 1)
                wait(sc, o_done, 2 * b)
                sc.activation(yt[:, 4 * half:4 * half + 4, HI, :],
                              y_bank[:, :].rearrange("p (g q) -> p g q", g=G), ACT.Copy).then_inc(y_hi, 1)

            def x2t_evac(b, par, r):
                wait(sc, x2t_done, 2 * b + r + 1)
                if r == 0:
                    wait(sc, ffn_done, 2 * (b - 2) + 2)
                sc.activation(xnt[par][:, HI, 4 * r:4 * r + 4, :],
                              x2t_bank[r][:, :].rearrange("p (k t) -> p k t", k=4), ACT.Copy,
                              scale=FFN_UP).then_inc(x2t_hi, 1)

            def ffn_weights(k):
                sc.activation(ffn_s[:, k, :], ffn_raw[:, k, :], ACT.Copy,
                              scale=ffn_sign[:, k:k + 1]).then_inc(ffn_ready, 1)

            for m in range(NKV // 2):
                q_out(N_BLK - 1, m)
            sc.wait_ge(wo_ready, KC // 2)
            for u in range(NKV):
                exps(0, u)
                if u:
                    pt_evac(0, u - 1)
                if u % 2:
                    q_out(N_BLK - 1, NKV // 2 + u // 2)
                if u == 4:
                    sc.wait_ge(const_made, 7)
                    sc.wait_ge(ffn_loaded, 16)
                if u >= 4:
                    ffn_weights(u - 4)

            def step(b, par, attn, t1, t2, first=False):
                for u in range(NKV):
                    if u == 6 and attn:
                        y_evac(b, 0)
                    if u == 0 and t1:
                        pt_evac(b - 1, 7)
                    if attn:
                        exps(b, u)
                    if u == 0 and t1:
                        if first:
                            y_evac(b - 1, 0)
                        y_evac(b - 1, 1)
                    if u == 7 and t1:
                        x2t_evac(b - 1, 1 - par, 0)
                        x2t_evac(b - 1, 1 - par, 1)
                    if u and attn:
                        pt_evac(b, u - 1)
                    if first and u < 4:
                        ffn_weights(4 + u)

            step(1, 1, True, True, False, first=True)
            step(2, 0, True, True, True)
            step(3, 1, True, True, True)
            with sc.Fori(2, N_BATCH // 2) as i:
                step(2 * i, 0, True, True, True)
                step(2 * i + 1, 1, True, True, True)
            step(N_BATCH, 0, False, True, True)

        @block.vector
        def _(dve):
            def c_split(n, k):
                wait(dve, c_hi, KC * n + k + 1)
                dve.tensor_tensor(act[0][:, k, LO, :], c_raw[k % CRING][:, :], act[0][:, k, HI, :].bitcast(F32),
                                  ALU.subtract).then_inc(c_ready, 1)

            def kv_out(n):
                for j in range(2):
                    wait(dve, k_hi, 2 * n + j + 1)
                    dve.scalar_tensor_tensor(
                        out=proj[j][:, :, LO, :], in0=bank[j][:, :].rearrange("p (b t) -> p b t", b=TPB),
                        scalar=bk_s[:, j:j + 1], in1=proj[j][:, :, HI, :].bitcast(F32),
                        op0=ALU.add, op1=ALU.subtract).then_inc(kv_evac, 1)
                for t in range(TPB):
                    wait(dve, kv_done, 6 * n + 3 + t)
                    wait(dve, v_stored, 16 * n)
                    dve.tensor_tensor(v_out[:, t, :], bank[2 + t][:, 0:KV], bv_s[:, :],
                                      ALU.add).then_inc(kv_evac, 1)

            for k in range(KC):
                c_split(0, k)
                wait(dve, wkv_hi, k + 1)
                dve.tensor_tensor(wkv_s[:, k, LO, :], w_raw[k % WRING][:, 0:2 * KV],
                                  wkv_s[:, k, HI, :].bitcast(F32), ALU.subtract).then_inc(wkv_ready, 1)
            dve.wait_ge(const_loaded, 16 * N_CONST_DMA)

            def kv_block(n):
                for k in range(2):
                    c_split(n, k)
                kv_out(n - 1)
                for k in range(2, KC):
                    c_split(n, k)

            kv_block(1)
            with dve.Fori(2, N_BLK - 1) as n:
                kv_block(n)

            def ln_stats(i, src):
                wait(dve, ln_rstd, i - 1)
                for h in range(2):
                    last = dve.bn_stats(st[:, h, :], src[:, h * 512:(h + 1) * 512])
                last.then_inc(ln_step, 1)

            def ln_settle(i):
                wait(dve, ln_step, i + 1)

            def ln_aggregate(par):
                dve.bn_aggr(mv[par][:, :], st[:, :, :].rearrange("p a b -> p (a b)")).then_inc(ln_var, 1)

            def ln_norm(i, par, src, dst, done):
                wait(dve, ln_rstd, i + 1)
                dve.tensor_scalar(dst, src, mv[par][:, 0:1], rstd[par][:, 0:1],
                                  ALU.subtract, ALU.mult).then_inc(done, 1)

            def x_stats(i):
                wait(dve, x_loaded[i % XRING], 16 * (i // XRING + 1))
                ln_stats(i, x_raw[i % XRING])
                ln_settle(i)
                ln_aggregate(i % 2)

            def x_norm(i):
                ln_norm(i, i % 2, x_raw[i % XRING][:, :], x_raw[i % XRING][:, :], xn_ready)

            def xt_out(i):
                n, t = i // TPB, i % TPB
                for r in range(2):
                    wait(dve, xt_hi, 2 * i + r + 1)
                    dst = act_of(n)
                    dve.tensor_tensor(dst[:, 4 * r:4 * r + 4, LO, t * P:(t + 1) * P],
                                      x_t[r][:, :].rearrange("p (k t) -> p k t", k=4),
                                      dst[:, 4 * r:4 * r + 4, HI, t * P:(t + 1) * P].bitcast(F32),
                                      ALU.subtract).then_inc(xt_ready, 1)

            for k in range(KC):
                c_split(N_BLK - 1, k)
                if k == 1:
                    x_stats(0)
                    x_norm(0)
                    x_stats(1)
                    kv_out(N_BLK - 2)
                if 3 <= k < 2 + TPB:
                    x_norm(k - 2)
                if 3 <= k < 1 + TPB:
                    x_stats(k - 1)
            for i in range(TPB):
                xt_out(i)
            kv_out(N_BLK - 1)
            x_stats(TPB)

            def q_out(n, m):
                wait(dve, q_hi, NKV * n + m + 1)
                dve.scalar_tensor_tensor(
                    out=proj[m % 2][:, :, LO, :], in0=bank[m % 4][:, :].rearrange("p (b t) -> p b t", b=TPB),
                    scalar=bq_s[:, m:m + 1], in1=proj[m % 2][:, :, HI, :].bitcast(F32),
                    op0=ALU.add, op1=ALU.subtract).then_inc(q_evac, 1)

            for n in range(N_BLK - 1):
                for m in range(NKV):
                    i = TPB * (n + 1) + m // 2
                    if m % 2 == 0:
                        x_norm(i)
                    elif i + 1 < N_TILE:
                        x_stats(i + 1)
                    q_out(n, m)
                    if m % 2 == 0:
                        xt_out(i)

            def row_max(b, u):
                wait(dve, qk_done, NKV * b + u + 1)
                dve.tensor_reduce(mx[u % 2][:, :], score[u % 2][:, :].rearrange("p (g k) -> p g k", g=G),
                                  AX, ALU.max).then_inc(max_done, 1)

            def neg_max(b, u):
                wait(dve, max_done, NKV * b + u + 1)
                dve.tensor_scalar(nb[u % 2][:, :], mx[u % 2][:, :], -SOFTMAX_SCALE, None,
                                  ALU.mult).then_inc(neg_max_ready, 1)

            def recip(b, u):
                wait(dve, exp_done, NKV * b + u + 1)
                dve.reciprocal(rsum[u % 2][:, :], sums[u % 2][:, :]).then_inc(rsum_ready, 1)

            def normalise(b, u):
                wait(dve, rsum_ready, NKV * b + u + 1)
                for g in range(G):
                    last = dve.tensor_scalar(pr[u % 2][:, g, :], pr[u % 2][:, g, :],
                                             rsum[u % 2][:, g:g + 1], None, ALU.mult)
                last.then_inc(prob_ready, 1)

            def y_out(b, half):
                wait(dve, y_hi, 2 * b + half + 1)
                dst = yt[:, 4 * half:4 * half + 4, :, :]
                dve.tensor_tensor(dst[:, :, LO, :], y_bank[:, :].rearrange("p (g q) -> p g q", g=G),
                                  dst[:, :, HI, :].bitcast(F32), ALU.subtract).then_inc(y_ready, 1)

            def x2_out(b, i, par, h):
                wait(dve, o_done, 2 * b + h + 1)
                wait(dve, xbo_ready, b + 1)
                wait(dve, out_stored[par], 16 * i)
                dve.tensor_tensor(x2[par][:, h * 512:(h + 1) * 512], o_bank[h][:, :],
                                  x_in[par][:, h * 512:(h + 1) * 512], ALU.add).then_inc(x2_ready, 1)

            def x2_stats(b, par, h):
                wait(dve, x2_ready, 2 * b + h + 1)
                if h == 0:
                    wait(dve, ln_rstd, N_TILE + b - 1)
                last = dve.bn_stats(st[:, h, :], x2[par][:, h * 512:(h + 1) * 512])
                if h == 1:
                    last.then_inc(ln_step, 1)
                    ln_settle(N_TILE + b)

            def x2_norm(b, par):
                wait(dve, x2t_done, 2 * b)
                ln_norm(N_TILE + b, par, x2[par][:, :], xn2[:, :], xn2_ready)

            def x2t_out(b, par, r):
                wait(dve, x2t_hi, 2 * b + r + 1)
                dve.scalar_tensor_tensor(
                    out=xnt[par][:, LO, 4 * r:4 * r + 4, :],
                    in0=x2t_bank[r][:, :].rearrange("p (k t) -> p k t", k=4),
                    scalar=FFN_UP, in1=xnt[par][:, HI, 4 * r:4 * r + 4, :],
                    op0=ALU.mult, op1=ALU.subtract).then_inc(x2t_ready, 1)

            def ffn_out(b, par, h):
                wait(dve, ffn_done, 2 * b + h + 1)
                cols = slice(h * 512, (h + 1) * 512)
                dve.scalar_tensor_tensor(out=x2[par][:, cols], in0=ffn_bank[h][:, :], scalar=scale_d[:, 0:1],
                                         in1=x2[par][:, cols], op0=ALU.mult, op1=ALU.add).then_inc(out_ready, 1)

            def unit(b, u, attn, prev):
                pb, pu = (b, u - 1) if u else (b - 1, NKV - 1)
                if prev:
                    recip(pb, pu)
                    normalise(pb, pu)
                if attn:
                    row_max(b, u)
                    neg_max(b, u)

            def step(b, i, par, attn, t1, t2, t3, first=False):
                for u in range(NKV):
                    if u == 4 and t1:
                        x2_out(b - 1, i - 1 + par, 1 - par, 0)
                        x2_stats(b - 1, 1 - par, 0)
                    if u == 6 and t1:
                        x2_out(b - 1, i - 1 + par, 1 - par, 1)
                        x2_stats(b - 1, 1 - par, 1)
                        if attn:
                            recip(b, 5)
                        ln_aggregate(1 - par)
                        if attn:
                            normalise(b, 5)
                            row_max(b, 6)
                            neg_max(b, 6)
                            y_out(b, 0)
                        x2_norm(b - 1, 1 - par)
                    else:
                        unit(b, u, attn, t1 if u == 0 else attn)
                    if u == 0 and t2:
                        x2t_out(b - 2, par, 0)
                        x2t_out(b - 2, par, 1)
                    if u == 0 and t3:
                        ffn_out(b - 3, 1 - par, 0)
                    if u == 0 and first:
                        y_out(b - 1, 0)
                    if u == 1 and t1:
                        y_out(b - 1, 1)
                    if u == 1 and t3:
                        ffn_out(b - 3, 1 - par, 1)

            for m in range(NKV // 2):
                q_out(N_BLK - 1, m)
            dve.wait_ge(const_made, 7)
            for u in range(NKV):
                unit(0, u, True, u > 0)
                if u % 2:
                    q_out(N_BLK - 1, NKV // 2 + u // 2)
            step(1, 0, 1, True, True, False, False, first=True)
            step(2, 1, 0, True, True, True, False)
            step(3, 1, 1, True, True, True, True)
            with dve.Fori(2, N_BATCH // 2) as i:
                step(2 * i, i, 0, True, True, True, True)
                step(2 * i + 1, i, 1, True, True, True, True)
            step(N_BATCH, N_BATCH // 2, 0, False, True, True, True)
            step(N_BATCH + 1, N_BATCH // 2, 1, False, False, True, True)
            step(N_BATCH + 2, N_BATCH // 2 + 1, 0, False, False, False, True)

        @block.tensor
        def _(pe):
            def kv_chunk(n, k, first_block):
                wait(pe, c_ready, KC * n + k + 1)
                if first_block:
                    wait(pe, wkv_ready, k + 1)
                a = act[0]
                for g in range(6):
                    if k == 0:
                        wait(pe, kv_evac, 6 * (n - 1) + g + 1)
                    for p, (w_part, a_part) in enumerate(((HI, HI), (HI, LO), (LO, HI))):
                        start, stop = k == 0 and p == 0, k == KC - 1 and p == 2
                        if g < 2:
                            last = pe.matmul(bank[g][:, :], wkv_s[:, k, w_part, g * P:(g + 1) * P],
                                             a[:, k, a_part, :], start=start, stop=stop)
                        else:
                            last = pe.matmul(bank[g][:, 0:KV], a[:, k, w_part, (g - 2) * P:(g - 1) * P],
                                             wkv_s[:, k, a_part, KV:2 * KV], start=start, stop=stop)
                    if k == KC - 1:
                        last.then_inc(kv_done, 1)
                if k < KC - 1:
                    last.then_inc(c_used, 1)

            def transpose_x(i):
                wait(pe, xn_ready, i + 1)
                for r in range(2):
                    wait(pe, xt_ready, 2 * (i - 1) + r + 1)
                    for k in range(4):
                        c = 4 * r + k
                        last = pe.transpose(x_t[r][:, k * P:(k + 1) * P],
                                            x_raw[i % XRING][:, c * P:(c + 1) * P], ident[:, :])
                    last.then_inc(xt_done, 1)

            def q_chunks(n, m, k0, k1):
                if k0 == 0:
                    wait(pe, q_evac, NKV * n + m - 3)
                    if n == 0 and m < 4:
                        wait(pe, kv_evac, 6 * (N_BLK - 1) + m + 1)
                for k in range(k0, k1):
                    for p, (w_part, a_part) in enumerate(((HI, HI), (HI, LO), (LO, HI))):
                        last = pe.matmul(bank[m % 4][:, :], wq_s[:, m, k, w_part, :],
                                         act_of(n)[:, k, a_part, :], start=k == 0 and p == 0,
                                         stop=k == KC - 1 and p == 2)
                if k1 == KC:
                    last.then_inc(q_done, 1)

            for k in range(KC):
                kv_chunk(0, k, True)
            with pe.Fori(1, N_BLK - 1) as n:
                for k in range(KC):
                    kv_chunk(n, k, False)
            pe.wait_ge(const_made, 6)
            for k in range(KC):
                kv_chunk(N_BLK - 1, k, False)
                if 3 <= k < 3 + TPB:
                    transpose_x(k - 3)
            pe.wait_ge(wq_ready, KC)
            for n in range(N_BLK - 1):
                wait(pe, xt_ready, 2 * TPB * (n + 1))
                for m in range(NKV):
                    q_chunks(n, m, 0, KC)
                    if m % 2 == 0:
                        transpose_x(TPB * (n + 1) + m // 2)

            def scores(b, i, par, u):
                if u == 0:
                    wait(pe, qv_loaded[par], 9 * 16 * (i + 1))
                if u % 4 == 0:
                    wait(pe, kd_loaded[u // 4], 4 * 16 * (b + 1))
                wait(pe, exp_done, NKV * b + u - 1)
                for pair in range(2):
                    for k_part in (HI, LO):
                        last = pe.matmul(score[u % 2][:, pair * 2 * P:(pair + 1) * 2 * P],
                                         q_s[par][:, u, pair, :], kd[:, u, k_part, :],
                                         start=k_part == HI, stop=k_part == LO)
                last.then_inc(qk_done, 1)

            def transpose_p(b, u):
                wait(pe, prob_ready, NKV * b + u + 1)
                wait(pe, pt_ready, NKV * b + u - 1)
                for g in range(G):
                    last = pe.transpose(prob_t[u % 2][:, g * P:(g + 1) * P], pr[u % 2][:, g, :], ident[:, :])
                last.then_inc(tp_done, 1)

            def attend(b, par, half):
                wait(pe, pt_ready, NKV * b + 4 * half + 4)
                wait(pe, y_ready, 2 * b + half)
                if half == 1:
                    wait(pe, x2t_ready, 2 * b)
                for c in range(4):
                    u = 4 * half + c
                    last = pe.matmul(y_bank[c * HD:(c + 1) * HD, :], v_s[par][:, u * HD:(u + 1) * HD],
                                     pt[:, u, :], start=True, stop=True)
                last.then_inc(pv_done, 1)

            def project(b, s0, s1):
                for s in range(s0, s1):
                    h, k = s // KC, s % KC
                    if s == 0:
                        wait(pe, y_ready, 2 * b + 1)
                        wait(pe, x2t_ready, 2 * b - 1)
                    if s == 4:
                        wait(pe, y_ready, 2 * b + 2)
                    if s == KC:
                        wait(pe, out_ready, 2 * (b - 2) + 2)
                    for p, (y_part, w_part) in enumerate(((HI, HI), (HI, LO), (LO, HI))):
                        last = pe.matmul(o_bank[h][:, :], yt[:, k, y_part, :],
                                         wo_chunk(k, w_part)[:, h * 512:(h + 1) * 512],
                                         start=k == 0 and p == 0, stop=k == KC - 1 and p == 2)
                    if k == KC - 1:
                        last.then_inc(o_done, 1)

            def transpose_x2(b, attn):
                wait(pe, xn2_ready, b + 1)
                wait(pe, y_ready, 2 * b + (3 if attn else 2))
                for r in range(2):
                    for k in range(4):
                        c = 4 * r + k
                        last = pe.transpose(x2t_bank[r][:, k * P:(k + 1) * P],
                                            xn2[:, c * P:(c + 1) * P], ident[:, :])
                    last.then_inc(x2t_done, 1)

            def ffn(b, par, s0, s1, projecting):
                for s in range(s0, s1):
                    h, k = s // KC, s % KC
                    if s == 0:
                        wait(pe, x2t_ready, 2 * b + 2)
                        wait(pe, out_ready, 2 * (b - 1) + 1)
                    if s == KC:
                        if projecting:
                            wait(pe, x2_ready, 2 * (b + 1) + 2)
                        else:
                            wait(pe, out_ready, 2 * (b - 1) + 2)
                    for part in (HI, LO):
                        last = pe.matmul(ffn_bank[h][:, :], xnt[par][:, part, k, :],
                                         ffn_s[:, k, h * 512:(h + 1) * 512],
                                         start=k == 0 and part == HI, stop=k == KC - 1 and part == LO)
                    if k == KC - 1:
                        last.then_inc(ffn_done, 1)

            O_AT = {1: (0, 3), 2: (3, 7), 3: (7, 10), 4: (10, 13), 5: (13, 16)}
            FFN_HEAD = 10

            def step(b, i, par, attn, t1, t2, t3, first=False):
                for u in range(NKV):
                    if attn:
                        scores(b, i, par, u)
                    if u == 0:
                        if t3:
                            ffn(b - 3, 1 - par, FFN_HEAD, 12, t1)
                        if t1:
                            transpose_p(b - 1, 7)
                        if t3:
                            ffn(b - 3, 1 - par, 12, 2 * KC, t1)
                        if first:
                            attend(b - 1, 1 - par, 0)
                        if t1:
                            attend(b - 1, 1 - par, 1)
                    if u in O_AT and t1:
                        project(b - 1, *O_AT[u])
                    if u == 6 and t2:
                        if not t3:
                            pe.wait_ge(ffn_ready, KC)
                        ffn(b - 2, par, 0, 5, t1)
                    if u == 7:
                        if t2:
                            ffn(b - 2, par, 5, 6, t1)
                        if t1:
                            transpose_x2(b - 1, attn)
                        if t2:
                            ffn(b - 2, par, 6, FFN_HEAD if t1 else 2 * KC, t1)
                    if u and attn:
                        transpose_p(b, u - 1)
                    if u == 5 and attn:
                        attend(b, par, 0)

            wait(pe, xt_ready, 2 * N_TILE)
            for m in range(NKV // 2):
                q_chunks(N_BLK - 1, m, 0, KC)
            for u in range(NKV):
                scores(0, 0, 0, u)
                h = KC // 2 * (u % 2)
                q_chunks(N_BLK - 1, NKV // 2 + u // 2, h, h + KC // 2)
                if u:
                    transpose_p(0, u - 1)
            pe.wait_ge(wo_ready, KC)
            pe.wait_ge(q_evac, NKV * N_BLK)
            step(1, 0, 1, True, True, False, False, first=True)
            step(2, 1, 0, True, True, True, False)
            step(3, 1, 1, True, True, True, True)
            with pe.Fori(2, N_BATCH // 2) as i:
                step(2 * i, i, 0, True, True, True, True)
                step(2 * i + 1, i, 1, True, True, True, True)
            step(N_BATCH, N_BATCH // 2, 0, False, True, True, True)
            step(N_BATCH + 1, N_BATCH // 2, 1, False, False, True, True)


def kernel(x, ctx_4096, L0_xattn_Wq, L0_xattn_bq, L0_xattn_Wk, L0_xattn_bk, L0_xattn_Wv, L0_xattn_bv,
           L0_xattn_Wo, L0_xattn_bo, L0_ffn_kernel, L0_ffn_scale):
    import numpy as np
    import concourse.bacc as bacc
    from concourse.bass_utils import run_bass_kernel_spmd

    wo_rows = np.asarray(L0_xattn_Wo).reshape(2, 4, G, HD, D).transpose(0, 2, 1, 3, 4).reshape(D, D)
    arrays = {
        "x": np.asarray(x).reshape(N_BATCH * P, D),
        "ctx_t": np.asarray(ctx_4096).reshape(N_BATCH * P, D).T,
        "wq": np.asarray(L0_xattn_Wq),
        "bq": np.asarray(L0_xattn_bq).reshape(KC, P).T,
        "wkv": np.concatenate([np.asarray(L0_xattn_Wk), np.asarray(L0_xattn_Wv)], axis=1),
        "bk": np.asarray(L0_xattn_bk).reshape(2, P).T,
        "bv": np.asarray(L0_xattn_bv),
        "wo": wo_rows,
        "bo": np.asarray(L0_xattn_bo),
        "ffn_w": np.asarray(L0_ffn_kernel),
        "ffn_scale": np.asarray(L0_ffn_scale).reshape(1),
    }
    arrays = {n: np.ascontiguousarray(a) for n, a in arrays.items()}
    nc = bacc.Bacc("TRN2", target_bir_lowering=False, num_devices=1)
    args = [nc.dram_tensor(n, a.shape, mybir.dt.from_np(a.dtype), kind="ExternalInput").ap()
            for n, a in arrays.items()]
    out = nc.dram_tensor("out", (N_BATCH * P, D), F32, kind="ExternalOutput").ap()
    attention_ffn(nc, *args, out)
    r = run_bass_kernel_spmd(nc, [arrays], core_ids=[0])
    return np.asarray(r.results[0]["out"]).reshape(N_BATCH, P, D)
```

```python
import concourse.bass as bass
from concourse import mybir

F32 = mybir.dt.float32
F32R = mybir.dt.float32r
F16 = mybir.dt.float16
U8 = mybir.dt.uint8
ALU = mybir.AluOpType
ACT = mybir.ActivationFunctionType
AX = mybir.AxisListType.X

P = 128
N_BATCH = 16
D = 1024
KC = D // P
BLK = 512
N_BLK = N_BATCH * P // BLK
TPB = BLK // P
HD = 32
NKV = 8
G = 4
KV = NKV * HD
HI, LO = 0, 1
EPS = 1e-5
SOFTMAX_SCALE = float(HD) ** -0.5
P_EXC = 0.8
N_EXC = round(D * P_EXC)
INHIBIT = -4.0
FFN_UP = 256.0
WRING = 3
CRING = 4
XRING = 4
KB = 1024


def wait(engine, semaphore, count):
    if isinstance(count, int) and count <= 0:
        return
    engine.wait_ge(semaphore, count)


def attention_ffn(nc, x, ctx_t, wq, bq, wkv, bk, bv, wo, bo, ffn_w, ffn_scale, out):
    base = (nc.sbuf_base + 31) // 32 * 32
    R_KV = base
    R_Q = R_KV + 32 * KB
    R_A1 = R_Q + 64 * KB
    R_A0 = R_A1 + 32 * KB
    R_W = R_A0 + 32 * KB
    R_C = R_W + WRING * 4 * KB
    R_O = R_C + CRING * 2 * KB
    R_S = R_O + 8 * KB
    R_END = R_S + 9 * KB

    def at(name, shape, dtype, offset):
        return nc.alloc_sbuf_tensor_at(name, shape, dtype, offset=offset)

    cursor = [R_END]

    def const(name, shape, dtype):
        size = 4
        for s in shape[1:]:
            size *= s
        t = at(name, shape, dtype, cursor[0])
        cursor[0] += (size + 31) // 32 * 32
        return t

    wkv_s = at("wkv_s", [P, KC, 2, 2 * KV], F32R, R_KV)
    wq_s = at("wq_s", [P, NKV, KC, 2, P], F32R, R_Q)
    act = [at(f"act{i}", [P, KC, 2, BLK], F32R, r) for i, r in ((0, R_A0), (1, R_A1))]
    w_raw = [at(f"w_raw{i}", [P, D], F32, R_W + i * 4 * KB) for i in range(WRING)]
    c_raw = [at(f"c_raw{i}", [P, BLK], F32, R_C + i * 2 * KB) for i in range(CRING)]
    x_raw = [at(f"x_raw{i}", [P, D], F32, R_W + i * 4 * KB if i < WRING else R_S + 4 * KB)
             for i in range(XRING)]
    proj = [at(f"proj{i}", [P, TPB, 2, P], F32R, R_O + i * 4 * KB) for i in range(2)]
    v_out = at("v_out", [P, TPB, KV], F32, R_S)
    wo_lo4 = at("wo_lo4", [P, KC // 2, 2, D], F32R, R_KV)
    wo_hi4 = at("wo_hi4", [P, KC // 2, 2, D], F32R, R_Q)
    ffn_s = at("ffn_s", [P, KC, D], F16, R_Q + 32 * KB)
    x_in = [at(f"x_in{i}", [P, D], F32, R_Q + (48 + 4 * i) * KB) for i in range(2)]
    x2 = [at(f"x2_{i}", [P, D], F32, R_Q + (56 + 4 * i) * KB) for i in range(2)]
    kd = at("kd", [P, NKV, 2, 2 * P], F32R, R_A1)
    ffn_raw = at("ffn_raw", [P, KC, D], U8, R_A1 + 16 * KB)
    wo_raw = [at(f"wo_raw{i}", [P, D], F32, r) for i, r in enumerate(
        (R_C, R_C + 4 * KB, R_A1 + 16 * KB, R_A1 + 20 * KB))]
    yt = at("yt", [P, KC, 2, P], F32R, R_A0)
    xn2 = at("xn2", [P, D], F32, R_A0 + 8 * KB)
    xnt = [at(f"xnt{i}", [P, 2, KC, P], F16, R_A0 + (12 + 4 * i) * KB) for i in range(2)]
    pr = [at(f"pr{i}", [P, G, P], F32, R_W + i * 2 * KB) for i in range(2)]
    pt = at("pt", [P, NKV, G * P], F32, R_W + 4 * KB)
    q_s = [at("q_s0", [P, NKV, 2, P], F32R, R_S), at("q_s1", [P, NKV, 2, P], F32R, R_A1 + 24 * KB)]
    v_s = [at("v_s0", [P, KV], F32, R_S + 8 * KB), const("v_s1", [P, KV], F32)]
    ident = const("ident", [P, P], F32)
    ffn_sign = const("ffn_sign", [P, KC], F32)
    bq_s = const("bq_s", [P, KC], F32)
    bk_s = const("bk_s", [P, 2], F32)
    bv_s = const("bv_s", [P, KV], F32)
    bo_s = const("bo_s", [P, D], F32)
    scale_s = const("scale_s", [P, 1], F32)
    scale_d = const("scale_d", [P, 1], F32)
    minus_half = const("minus_half", [P, 1], F32)
    eps_s = const("eps_s", [P, 1], F32)
    st = const("st", [P, 2, 6], F32)
    mv = [const(f"mv{i}", [P, 2], F32) for i in range(2)]
    ve = const("ve", [P, 1], F32)
    rstd = [const(f"rstd{i}", [P, 1], F32) for i in range(2)]
    mx = [const(f"mx{i}", [P, G], F32) for i in range(2)]
    nb = [const(f"nb{i}", [P, G], F32) for i in range(2)]
    sums = [const(f"sums{i}", [P, G], F32) for i in range(2)]
    rsum = [const(f"rsum{i}", [P, G], F32) for i in range(2)]
    assert cursor[0] <= nc.sbuf_usable_end, (cursor[0], nc.sbuf_usable_end)

    bank = [nc.alloc_psum_tensor(f"bank{i}", [P, 512], F32) for i in range(8)]
    score, prob_t, x_t = bank[4:6], bank[6:8], bank[6:8]
    y_bank = bank[2]
    o_bank = [bank[0], bank[1]]
    x2t_bank = [bank[0], bank[2]]
    x2t_bank0 = [bank[3], bank[2]]
    ffn_bank = [bank[3], bank[1]]

    q_d = nc.dram_tensor("q_d", [N_BATCH, P, NKV, 2, P], F32)
    k_d = nc.dram_tensor("k_d", [N_BATCH, HD, NKV, 2, P], F32)
    v_d = nc.dram_tensor("v_d", [N_BATCH, P, KV], F32)

    S = {n: nc.alloc_semaphore(n) for n in (
        "const_loaded", "const_made", "c_loaded0", "c_loaded1", "c_loaded2", "c_loaded3",
        "wkv_loaded0", "wkv_loaded1", "wkv_loaded2",
        "wkv_hi", "wkv_ready", "c_hi", "c_ready", "c_used", "kv_done", "k_hi", "kv_evac",
        "k_stored", "v_stored", "wq_loaded0", "wq_loaded1", "wq_loaded2", "wq_hi", "wq_ready",
        "x_loaded0", "x_loaded1", "x_loaded2", "x_loaded3", "ln_step", "ln_var", "ln_ve",
        "ln_rstd", "xn_ready", "xt_done", "xt_hi", "xt_ready", "q_done", "q_hi", "q_evac",
        "q_stored0", "q_stored1", "wo_loaded0", "wo_loaded1", "wo_hi", "wo_ready",
        "ffn_loaded", "ffn_ready", "kd_zeroed",
        "kd_loaded0", "kd_loaded1", "qv_loaded0", "qv_loaded1", "x_in_loaded0", "x_in_loaded1",
        "qk_done", "max_done", "neg_max_ready", "exp_done", "rsum_ready", "prob_ready", "tp_done",
        "pt_ready", "pv_done", "y_hi", "y_ready", "xbo_ready", "o_done", "x2_ready",
        "xn2_ready", "x2t_done", "x2t_hi", "x2t_ready", "ffn_done", "out_ready", "y0_used",
        "out_stored0", "out_stored1")}
    (const_loaded, const_made, wkv_hi, wkv_ready, c_hi, c_ready, c_used, kv_done, k_hi, kv_evac,
     k_stored, v_stored, wq_hi, wq_ready, ln_step, ln_var, ln_ve, ln_rstd, xn_ready, xt_done,
     xt_hi, xt_ready, q_done, q_hi, q_evac, wo_hi, wo_ready, ffn_loaded, ffn_ready, kd_zeroed,
     qk_done, max_done, neg_max_ready, exp_done, rsum_ready, prob_ready, tp_done, pt_ready,
     pv_done, y_hi, y_ready, xbo_ready, o_done, x2_ready, xn2_ready, x2t_done, x2t_hi,
     x2t_ready, ffn_done, out_ready, y0_used) = (S[n] for n in (
         "const_loaded", "const_made", "wkv_hi", "wkv_ready", "c_hi", "c_ready", "c_used",
         "kv_done", "k_hi", "kv_evac", "k_stored", "v_stored", "wq_hi", "wq_ready", "ln_step",
         "ln_var", "ln_ve", "ln_rstd", "xn_ready", "xt_done", "xt_hi", "xt_ready", "q_done",
         "q_hi", "q_evac", "wo_hi", "wo_ready", "ffn_loaded", "ffn_ready", "kd_zeroed",
         "qk_done", "max_done", "neg_max_ready", "exp_done", "rsum_ready", "prob_ready",
         "tp_done", "pt_ready", "pv_done", "y_hi", "y_ready", "xbo_ready", "o_done", "x2_ready",
         "xn2_ready", "x2t_done", "x2t_hi", "x2t_ready", "ffn_done", "out_ready",
         "y0_used"))
    c_loaded = [S[f"c_loaded{i}"] for i in range(CRING)]
    wkv_loaded = [S[f"wkv_loaded{i}"] for i in range(WRING)]
    wq_loaded = [S[f"wq_loaded{i}"] for i in range(WRING)]
    x_loaded = [S[f"x_loaded{i}"] for i in range(XRING)]
    wo_loaded = [S["wo_loaded0"], S["wo_loaded1"]]
    q_stored = [S["q_stored0"], S["q_stored1"]]
    kd_loaded = [S["kd_loaded0"], S["kd_loaded1"]]
    qv_loaded = [S["qv_loaded0"], S["qv_loaded1"]]
    x_in_loaded = [S["x_in_loaded0"], S["x_in_loaded1"]]
    out_stored = [S["out_stored0"], S["out_stored1"]]

    Q_END = (4, 7, 11, 14, 17, 20, 23, 26)
    Q_LATE = {0: (27, 28), 1: (28, 29), 2: (29, 30), 7: (30, 32)}
    Q_HI_AT, Q_LO_AT = {3: 4, 5: 5, 7: 6}, {4: 4, 6: 5, 7: 6}
    N_CONST_DMA = 5
    N_TILE = N_BATCH
    block = nc.Block()

    def wo_chunk(kk, part):
        half = wo_lo4 if kk < KC // 2 else wo_hi4
        return half[:, kk % (KC // 2), part, :]

    def act_of(n):
        return act[(n + 1) % 2]

    with block:

        @block.sync
        def _(sp):
            def load_c(n, k):
                wait(sp, c_ready, KC * n + k + 1 - CRING)
                sp.dma_start(c_raw[k % CRING][:, :],
                             ctx_t[k * P:(k + 1) * P, bass.ds(n * BLK, BLK)]).then_inc(c_loaded[k % CRING], 16)

            def store_kv(n):
                for j in range(2):
                    wait(sp, kv_evac, 6 * n + j + 1)
                    for c in range(4):
                        sp.dma_start(
                            k_d[bass.ds(n * TPB, TPB), :, 4 * j + c, :, :].rearrange("b d h t -> d b (h t)"),
                            proj[j][c * HD:(c + 1) * HD, :, :, :].rearrange("d b h t -> d b (h t)").bitcast(F32),
                        ).then_inc(k_stored, 16)
                wait(sp, kv_evac, 6 * n + 6)
                sp.dma_start(v_d[bass.ds(n * TPB, TPB), :, :].rearrange("b p v -> p b v"),
                             v_out[:, :, :]).then_inc(v_stored, 16)

            for k in range(KC):
                load_c(0, k)
                wait(sp, wkv_ready, k + 1 - WRING)
                sp.dma_start(w_raw[k % WRING][:, 0:2 * KV],
                             wkv[k * P:(k + 1) * P, :]).then_inc(wkv_loaded[k % WRING], 16)
                if k == 1:
                    sp.dma_start(bq_s[:, :], bq).then_inc(const_loaded, 16)
                    sp.dma_start(bk_s[:, :], bk).then_inc(const_loaded, 16)
                    sp.dma_start(bv_s[:, :], bv.partition_broadcast(P)).then_inc(const_loaded, 16)
                    sp.dma_start(bo_s[:, :], bo.partition_broadcast(P)).then_inc(const_loaded, 16)
                    sp.dma_start(scale_s[:, :], ffn_scale.partition_broadcast(P)).then_inc(const_loaded, 16)
            with sp.Fori(1, N_BLK - 1) as n:
                for k in range(KC):
                    load_c(n, k)
                store_kv(n - 1)

            def load_x(i):
                wait(sp, xt_done, 2 * (i - XRING + 1))
                sp.dma_start(x_raw[i % XRING][:, :],
                             x[i * P:(i + 1) * P, :]).then_inc(x_loaded[i % XRING], 16)

            wait(sp, wq_ready, KC)
            for k in range(KC):
                if k % 2 == 0:
                    load_x(k // 2)
                load_c(N_BLK - 1, k)
            store_kv(N_BLK - 2)
            for i in range(XRING, 2 * XRING):
                load_x(i)
            store_kv(N_BLK - 1)

            def store_q(n, m):
                wait(sp, q_evac, NKV * n + m + 1)
                sp.dma_start(
                    q_d[n * TPB:(n + 1) * TPB, :, m, :, :].rearrange("b p h t -> p b (h t)"),
                    proj[m % 2][:, :, :, :].rearrange("p b h t -> p b (h t)").bitcast(F32),
                ).then_inc(q_stored[m % 2], 16)

            def load_kd(b, half):
                for e in range(2):
                    for part in range(2):
                        row = (2 * e + part) * HD
                        sp.dma_start(
                            kd[row:row + HD, 4 * half:4 * half + 4, :, e * P:(e + 1) * P]
                            .rearrange("p c h t -> p (c h) t").bitcast(F32),
                            k_d[b, :, 4 * half:4 * half + 4, :, :].rearrange("d c h t -> d (c h) t"),
                        ).then_inc(kd_loaded[half], 16)

            def load_qv(b, par):
                for e in range(2):
                    for part in range(2):
                        row = (2 * e + part) * HD
                        for pair in range(2):
                            g = 2 * pair + e
                            sp.dma_start(q_s[par][row:row + HD, :, pair, :].bitcast(F32),
                                         q_d[b, g * HD:(g + 1) * HD, :, part, :]).then_inc(qv_loaded[par], 16)
                sp.dma_start(v_s[par][:, :], v_d[b]).then_inc(qv_loaded[par], 16)

            def load_x_in(b, par):
                sp.dma_start(x_in[par][:, :], x[bass.ds(b * P, P), :]).then_inc(x_in_loaded[par], 16)

            for n in range(N_BLK):
                for m in range(NKV):
                    if n == N_BLK - 1 and m == 0:
                        wait(sp, k_stored, 8 * 16 * N_BLK)
                        wait(sp, v_stored, 16 * N_BLK)
                        wait(sp, q_done, NKV * (N_BLK - 1))
                        load_kd(0, 0)
                        wait(sp, q_stored[0], 16 * 4)
                        wait(sp, q_stored[1], 16 * 4)
                        wait(sp, xt_done, 2 * N_TILE)
                        load_qv(0, 0)
                    if n == N_BLK - 1 and m == NKV - 1:
                        wait(sp, qk_done, NKV)
                        load_kd(1, 1)
                        continue
                    store_q(n, m)
                    if n == N_BLK - 1 and m == 0:
                        load_kd(0, 1)
                    if n == N_BLK - 1 and m == 2:
                        load_qv(1, 1)
                    if m % 2 == 0 and n < N_BLK - 2:
                        load_x(4 * (n + 2) + m // 2)
                    if n == N_BLK - 1 and m == 4:
                        wait(sp, qk_done, 4)
                        load_kd(1, 0)
                    if n == N_BLK - 1 and m == 6:
                        load_x_in(0, 0)

            def step(b, i, par, attn, more, t3):
                if attn:
                    wait(sp, x2_ready, 2 * (b - 2) + 2)
                    load_x_in(b, par)
                if t3:
                    wait(sp, out_ready, 2 * (b - 3) + 2)
                    sp.dma_start(out[bass.ds((b - 3) * P, P), :], x2[1 - par][:, :]).then_inc(out_stored[1 - par], 16)
                if more:
                    wait(sp, pv_done, 2 * b)
                    load_qv(b + 1, 1 - par)
                    wait(sp, qk_done, NKV * b + 4)
                    load_kd(b + 1, 0)
                    wait(sp, qk_done, NKV * b + 8)
                    load_kd(b + 1, 1)

            step(1, 0, 1, True, True, False)
            store_q(N_BLK - 1, NKV - 1)
            step(2, 1, 0, True, True, False)
            wait(sp, q_stored[0], 16 * 4 * N_BLK)
            wait(sp, q_stored[1], 16 * 4 * N_BLK)
            step(3, 1, 1, True, True, True)
            last = N_BATCH // 2 - 1
            with sp.Fori(2, last) as i:
                step(2 * i, i, 0, True, True, True)
                step(2 * i + 1, i, 1, True, True, True)
            step(2 * last, last, 0, True, True, True)
            step(2 * last + 1, last, 1, True, False, True)
            step(N_BATCH, last + 1, 0, False, False, True)
            step(N_BATCH + 1, last + 1, 1, False, False, True)
            for h in range(2):
                wait(sp, out_ready, 2 * (N_BATCH - 1) + h + 1)
                sp.dma_start(out[(N_BATCH - 1) * P:N_BATCH * P, h * 512:(h + 1) * 512],
                             x2[1][:, h * 512:(h + 1) * 512]).then_inc(out_stored[1], 16)
            wait(sp, out_stored[0], 16 * N_BATCH // 2)
            wait(sp, out_stored[1], 16 * (N_BATCH // 2 + 1))

        @block.gpsimd
        def _(pool):
            pool.memset(ident[:, :], 0.0).then_inc(const_made, 1)
            pool.memset(ffn_sign[:, :], 1.0).then_inc(const_made, 1)
            pool.memset(minus_half[:, :], -0.5).then_inc(const_made, 1)
            pool.memset(eps_s[:, :], EPS).then_inc(const_made, 1)
            pool.wait_ge(const_made, 4)
            pool.affine_select(out=ident[:, :], in_=ident[:, :], compare_op=ALU.not_equal, fill=1.0,
                               base=0, pattern=[[-1, P]], channel_multiplier=1).then_inc(const_made, 1)
            pool.affine_select(out=ffn_sign[:, :], in_=ffn_sign[:, :], compare_op=ALU.is_ge, fill=INHIBIT,
                               base=N_EXC - 1, pattern=[[-P, KC]], channel_multiplier=-1).then_inc(const_made, 1)
            pool.wait_ge(const_made, 6)
            pool.wait_ge(const_loaded, 16 * N_CONST_DMA)
            pool.tensor_scalar(scale_d[:, :], scale_s[:, :], 1.0 / FFN_UP, None, ALU.mult).then_inc(const_made, 1)

            def load_wq(k):
                if k < WRING:
                    pool.wait_ge(wkv_ready, KC)
                else:
                    pool.wait_ge(wq_ready, k - WRING + 1)
                pool.dma_start(w_raw[k % WRING][:, :], wq[k * P:(k + 1) * P, :]).then_inc(wq_loaded[k % WRING], 16)

            for k in range(WRING - 1):
                load_wq(k)
            for k in range(KC):
                if k + WRING - 1 < KC:
                    load_wq(k + WRING - 1)
                raw = w_raw[k % WRING][:, :].rearrange("p (m c) -> p m c", m=NKV)
                pool.wait_ge(wq_hi, k + 1)
                pool.tensor_tensor(wq_s[:, :, k, LO, :], raw, wq_s[:, :, k, HI, :].bitcast(F32),
                                   ALU.subtract).then_inc(wq_ready, 1)

            def inv_std(i, par):
                wait(pool, ln_var, i + 1)
                pool.tensor_tensor(ve[:, :], mv[par][:, 1:2], eps_s[:, :], ALU.add).then_inc(ln_ve, 1)
                wait(pool, ln_ve, i + 1)
                pool.tensor_tensor(rstd[par][:, :], ve[:, :], minus_half[:, :], ALU.pow).then_inc(ln_rstd, 1)

            def wo_slot(k):
                return wo_raw[k % 2 + 2 * (k // 4)]

            def load_wo(k):
                if k == 0:
                    pool.wait_ge(c_ready, KC * N_BLK)
                if k == 4:
                    pool.wait_ge(q_done, NKV * (N_BLK - 1))
                if k % 4 >= 2:
                    pool.wait_ge(wo_ready, k - 1)
                pool.dma_start(wo_slot(k)[:, :], wo[k * P:(k + 1) * P, :]).then_inc(wo_loaded[k % 2], 16)

            def split_wo(k):
                pool.wait_ge(wo_loaded[k % 2], 16 * (k // 2 + 1))
                if k == 0:
                    pool.wait_ge(kv_done, 6 * N_BLK)
                if k >= KC // 2:
                    pool.wait_ge(q_done, NKV * (N_BLK - 1) + k - 3)
                pool.tensor_copy(wo_chunk(k, HI), wo_slot(k)[:, :]).then_inc(wo_hi, 1)
                pool.wait_ge(wo_hi, k + 1)
                pool.tensor_tensor(wo_chunk(k, LO), wo_slot(k)[:, :], wo_chunk(k, HI).bitcast(F32),
                                   ALU.subtract).then_inc(wo_ready, 1)
                if k % 4 < 2:
                    load_wo(k + 2)

            for i in range(5):
                inv_std(i, i % 2)
            load_wo(0)
            load_wo(1)
            for i in range(5, N_TILE):
                inv_std(i, i % 2)
                if i - 5 < KC // 2:
                    split_wo(i - 5)
            pool.wait_ge(q_done, NKV * (N_BLK - 1))
            for e in range(2):
                pool.memset(kd[e * 2 * HD:(e + 1) * 2 * HD, :, :, (1 - e) * P:(2 - e) * P]
                            .rearrange("p a b c -> p (a b) c").bitcast(F32), 0.0).then_inc(kd_zeroed, 1)
                pool.wait_ge(kd_zeroed, e + 1)

            def add_bo(b, i, par):
                wait(pool, x_in_loaded[par], 16 * (i + 1))
                pool.tensor_tensor(x_in[par][:, :], x_in[par][:, :], bo_s[:, :], ALU.add).then_inc(xbo_ready, 1)

            load_wo(4)
            load_wo(5)
            for k in range(KC // 2, KC):
                split_wo(k)
            pool.wait_ge(wo_ready, KC)
            pool.dma_start(ffn_raw[:, :, :], ffn_w.rearrange("(k p) n -> p k n", p=P)).then_inc(ffn_loaded, 16)
            pool.wait_ge(q_done, NKV * (N_BLK - 1) + 6)
            pool.wait_ge(ffn_loaded, 16)
            for k in range(KC):
                pool.tensor_scalar(ffn_s[:, k, :], ffn_raw[:, k, :], ffn_sign[:, k:k + 1], None,
                                   ALU.mult).then_inc(ffn_ready, 1)
                if k == KC // 2:
                    add_bo(0, 0, 0)
            add_bo(1, 0, 1)
            inv_std(N_TILE, 0)
            add_bo(2, 1, 0)
            inv_std(N_TILE + 1, 1)
            add_bo(3, 1, 1)
            inv_std(N_TILE + 2, 0)
            with pool.Fori(2, N_BATCH // 2) as i:
                add_bo(2 * i, i, 0)
                inv_std(N_TILE + 2 * i - 1, 1)
                add_bo(2 * i + 1, i, 1)
                inv_std(N_TILE + 2 * i, 0)
            inv_std(N_TILE + N_BATCH - 1, 1)

        @block.scalar
        def _(sc):
            def c_split(n, k):
                wait(sc, c_loaded[k % CRING], 16 * (2 * n + k // CRING + 1))
                if k < KC - 1:
                    wait(sc, c_used, (KC - 1) * (n - 1) + k + 1)
                else:
                    wait(sc, kv_done, 6 * n)
                sc.activation(act[0][:, k, HI, :], c_raw[k % CRING][:, :], ACT.Copy).then_inc(c_hi, 1)

            def k_evac(n):
                for j in range(2):
                    wait(sc, kv_done, 6 * n + j + 1)
                    wait(sc, k_stored, 8 * 16 * n)
                    sc.activation(proj[j][:, :, HI, :], bank[j][:, :].rearrange("p (b t) -> p b t", b=TPB),
                                  ACT.Identity, bias=bk_s[:, j:j + 1]).then_inc(k_hi, 1)

            for k in range(KC):
                c_split(0, k)
                sc.wait_ge(wkv_loaded[k % WRING], 16 * (k // WRING + 1))
                sc.activation(wkv_s[:, k, HI, :], w_raw[k % WRING][:, 0:2 * KV], ACT.Copy).then_inc(wkv_hi, 1)
            sc.wait_ge(const_loaded, 16 * N_CONST_DMA)

            def wq_split(k):
                sc.wait_ge(wq_loaded[k % WRING], 16 * (k // WRING + 1))
                sc.activation(wq_s[:, :, k, HI, :], w_raw[k % WRING][:, :].rearrange("p (m c) -> p m c", m=NKV),
                              ACT.Copy).then_inc(wq_hi, 1)

            def kv_block(n, with_wq=False):
                for k in range(KC):
                    c_split(n, k)
                    if with_wq:
                        wq_split(k)
                    if k == 1:
                        k_evac(n - 1)

            kv_block(1, with_wq=True)
            with sc.Fori(2, N_BLK - 1) as n:
                kv_block(n)

            def xt_evac(i):
                n, t = i // TPB, i % TPB
                for r in range(2):
                    wait(sc, xt_done, 2 * i + r + 1)
                    wait(sc, q_done, NKV * (n - 1))
                    sc.activation(act_of(n)[:, 4 * r:4 * r + 4, HI, t * P:(t + 1) * P],
                                  x_t[r][:, :].rearrange("p (k t) -> p k t", k=4), ACT.Copy).then_inc(xt_hi, 1)

            for k in range(KC):
                c_split(N_BLK - 1, k)
                if k == 1:
                    k_evac(N_BLK - 2)
            for i in range(TPB):
                xt_evac(i)
            k_evac(N_BLK - 1)

            def q_out(n, m):
                wait(sc, q_done, NKV * n + m + 1)
                if n == 0:
                    wait(sc, k_stored, 8 * 16 * N_BLK)
                wait(sc, q_stored[m % 2], 16 * (4 * n + m // 2))
                sc.activation(proj[m % 2][:, :, HI, :], bank[m % 4][:, :].rearrange("p (b t) -> p b t", b=TPB),
                              ACT.Identity, bias=bq_s[:, m:m + 1]).then_inc(q_hi, 1)

            for n in range(N_BLK - 1):
                for m in range(NKV):
                    q_out(n, m)
                    if m % 2 == 0:
                        xt_evac(TPB * (n + 1) + m // 2)

            def exps(b, u):
                par = u % 2
                wait(sc, neg_max_ready, NKV * b + u + 1)
                wait(sc, tp_done, NKV * b + u - 1)
                for g in range(G):
                    last = sc.activation(pr[par][:, g, :], score[par][:, g * P:(g + 1) * P], ACT.Exp,
                                         bias=nb[par][:, g:g + 1], scale=SOFTMAX_SCALE,
                                         accum_out=sums[par][:, g:g + 1])
                last.then_inc(exp_done, 1)

            def pt_evac(b, u):
                wait(sc, tp_done, NKV * b + u + 1)
                wait(sc, pv_done, 2 * (b - 1) + u // 4 + 1)
                sc.activation(pt[:, u, :], prob_t[u % 2][:, :], ACT.Copy).then_inc(pt_ready, 1)

            def y_evac(b, half):
                wait(sc, pv_done, 2 * b + half + 1)
                if isinstance(b, int) and b == 1 and half == 0:
                    wait(sc, y0_used, 1)
                else:
                    wait(sc, o_done, 2 * b)
                sc.activation(yt[:, 4 * half:4 * half + 4, HI, :],
                              y_bank[:, :].rearrange("p (g q) -> p g q", g=G), ACT.Copy).then_inc(y_hi, 1)

            def x2t_evac(b, par, r, banks=x2t_bank):
                wait(sc, x2t_done, 2 * b + r + 1)
                if r == 0:
                    wait(sc, ffn_done, 2 * (b - 2) + 2)
                sc.activation(xnt[par][:, HI, 4 * r:4 * r + 4, :],
                              banks[r][:, :].rearrange("p (k t) -> p k t", k=4), ACT.Copy,
                              scale=FFN_UP).then_inc(x2t_hi, 1)

            for m in range(NKV // 2 - 1):
                q_out(N_BLK - 1, m)
            sc.wait_ge(wo_ready, KC // 2)
            for u in range(NKV):
                exps(0, u)
                if u == 0:
                    q_out(N_BLK - 1, NKV // 2 - 1)
                if u in Q_HI_AT:
                    q_out(N_BLK - 1, Q_HI_AT[u])
                if u:
                    pt_evac(0, u - 1)

            def step(b, par, attn, t1, t2, first=False, second=False):
                for u in range(NKV):
                    if u == 6 and attn and not first:
                        y_evac(b, 0)
                    if u == 1 and t1:
                        y_evac(b - 1, 1)
                    if attn:
                        exps(b, u)
                    if u == 0 and first:
                        y_evac(b - 1, 0)
                    if u == 0 and t1:
                        pt_evac(b - 1, 7)
                    if u == 0 and second:
                        q_out(N_BLK - 1, NKV - 1)
                    if u == 3 and second:
                        x2t_evac(b - 2, par, 0, x2t_bank0)
                        x2t_evac(b - 2, par, 1, x2t_bank0)
                    if u == 7 and first:
                        y_evac(b, 0)
                    if u == 7 and t1 and not first:
                        x2t_evac(b - 1, 1 - par, 0)
                        x2t_evac(b - 1, 1 - par, 1)
                    if u and attn:
                        pt_evac(b, u - 1)

            step(1, 1, True, True, False, first=True)
            step(2, 0, True, True, True, second=True)
            step(3, 1, True, True, True)
            with sc.Fori(2, N_BATCH // 2) as i:
                step(2 * i, 0, True, True, True)
                step(2 * i + 1, 1, True, True, True)
            step(N_BATCH, 0, False, True, True)

        @block.vector
        def _(dve):
            def c_split(n, k):
                wait(dve, c_hi, KC * n + k + 1)
                dve.tensor_tensor(act[0][:, k, LO, :], c_raw[k % CRING][:, :], act[0][:, k, HI, :].bitcast(F32),
                                  ALU.subtract).then_inc(c_ready, 1)

            def kv_out(n):
                for j in range(2):
                    wait(dve, k_hi, 2 * n + j + 1)
                    dve.scalar_tensor_tensor(
                        out=proj[j][:, :, LO, :], in0=bank[j][:, :].rearrange("p (b t) -> p b t", b=TPB),
                        scalar=bk_s[:, j:j + 1], in1=proj[j][:, :, HI, :].bitcast(F32),
                        op0=ALU.add, op1=ALU.subtract).then_inc(kv_evac, 1)
                for t in range(TPB):
                    wait(dve, kv_done, 6 * n + 3 + t)
                    wait(dve, v_stored, 16 * n)
                    dve.tensor_tensor(v_out[:, t, :], bank[2 + t][:, 0:KV], bv_s[:, :],
                                      ALU.add).then_inc(kv_evac, 1)

            for k in range(KC):
                c_split(0, k)
                wait(dve, wkv_hi, k + 1)
                dve.tensor_tensor(wkv_s[:, k, LO, :], w_raw[k % WRING][:, 0:2 * KV],
                                  wkv_s[:, k, HI, :].bitcast(F32), ALU.subtract).then_inc(wkv_ready, 1)
            dve.wait_ge(const_loaded, 16 * N_CONST_DMA)

            def kv_block(n):
                for k in range(2):
                    c_split(n, k)
                kv_out(n - 1)
                for k in range(2, KC):
                    c_split(n, k)

            kv_block(1)
            with dve.Fori(2, N_BLK - 1) as n:
                kv_block(n)

            def ln_stats(i, src):
                wait(dve, ln_rstd, i - 1)
                for h in range(2):
                    last = dve.bn_stats(st[:, h, :], src[:, h * 512:(h + 1) * 512])
                last.then_inc(ln_step, 1)

            def ln_settle(i):
                wait(dve, ln_step, i + 1)

            def ln_aggregate(par):
                dve.bn_aggr(mv[par][:, :], st[:, :, :].rearrange("p a b -> p (a b)")).then_inc(ln_var, 1)

            def ln_norm(i, par, src, dst, done):
                wait(dve, ln_rstd, i + 1)
                dve.tensor_scalar(dst, src, mv[par][:, 0:1], rstd[par][:, 0:1],
                                  ALU.subtract, ALU.mult).then_inc(done, 1)

            def x_stats(i):
                wait(dve, x_loaded[i % XRING], 16 * (i // XRING + 1))
                ln_stats(i, x_raw[i % XRING])
                ln_settle(i)
                ln_aggregate(i % 2)

            def x_norm(i):
                ln_norm(i, i % 2, x_raw[i % XRING][:, :], x_raw[i % XRING][:, :], xn_ready)

            def xt_out(i):
                n, t = i // TPB, i % TPB
                for r in range(2):
                    wait(dve, xt_hi, 2 * i + r + 1)
                    dst = act_of(n)
                    dve.tensor_tensor(dst[:, 4 * r:4 * r + 4, LO, t * P:(t + 1) * P],
                                      x_t[r][:, :].rearrange("p (k t) -> p k t", k=4),
                                      dst[:, 4 * r:4 * r + 4, HI, t * P:(t + 1) * P].bitcast(F32),
                                      ALU.subtract).then_inc(xt_ready, 1)

            for k in range(KC):
                c_split(N_BLK - 1, k)
                if k == 1:
                    x_stats(0)
                    x_norm(0)
                    kv_out(N_BLK - 2)
                    x_stats(1)
                if 3 <= k < 2 + TPB:
                    x_norm(k - 2)
                if 3 <= k < 1 + TPB:
                    x_stats(k - 1)
            for i in range(TPB):
                xt_out(i)
            kv_out(N_BLK - 1)
            x_stats(TPB)

            def q_out(n, m):
                wait(dve, q_hi, NKV * n + m + 1)
                dve.scalar_tensor_tensor(
                    out=proj[m % 2][:, :, LO, :], in0=bank[m % 4][:, :].rearrange("p (b t) -> p b t", b=TPB),
                    scalar=bq_s[:, m:m + 1], in1=proj[m % 2][:, :, HI, :].bitcast(F32),
                    op0=ALU.add, op1=ALU.subtract).then_inc(q_evac, 1)

            for n in range(N_BLK - 1):
                for m in range(NKV):
                    i = TPB * (n + 1) + m // 2
                    if m % 2 == 0:
                        x_norm(i)
                    elif i + 1 < N_TILE:
                        x_stats(i + 1)
                    q_out(n, m)
                    if m % 2 == 0:
                        xt_out(i)

            def row_max(b, u):
                wait(dve, qk_done, NKV * b + u + 1)
                dve.tensor_reduce(mx[u % 2][:, :], score[u % 2][:, :].rearrange("p (g k) -> p g k", g=G),
                                  AX, ALU.max).then_inc(max_done, 1)

            def neg_max(b, u):
                wait(dve, max_done, NKV * b + u + 1)
                dve.tensor_scalar(nb[u % 2][:, :], mx[u % 2][:, :], -SOFTMAX_SCALE, None,
                                  ALU.mult).then_inc(neg_max_ready, 1)

            def recip(b, u):
                wait(dve, exp_done, NKV * b + u + 1)
                dve.reciprocal(rsum[u % 2][:, :], sums[u % 2][:, :]).then_inc(rsum_ready, 1)

            def normalise(b, u):
                wait(dve, rsum_ready, NKV * b + u + 1)
                for g in range(G):
                    last = dve.tensor_scalar(pr[u % 2][:, g, :], pr[u % 2][:, g, :],
                                             rsum[u % 2][:, g:g + 1], None, ALU.mult)
                last.then_inc(prob_ready, 1)

            def y_out(b, half):
                wait(dve, y_hi, 2 * b + half + 1)
                dst = yt[:, 4 * half:4 * half + 4, :, :]
                dve.tensor_tensor(dst[:, :, LO, :], y_bank[:, :].rearrange("p (g q) -> p g q", g=G),
                                  dst[:, :, HI, :].bitcast(F32), ALU.subtract).then_inc(y_ready, 1)

            def x2_out(b, i, par, h):
                wait(dve, o_done, 2 * b + h + 1)
                wait(dve, xbo_ready, b + 1)
                wait(dve, out_stored[par], 16 * i)
                dve.tensor_tensor(x2[par][:, h * 512:(h + 1) * 512], o_bank[h][:, :],
                                  x_in[par][:, h * 512:(h + 1) * 512], ALU.add).then_inc(x2_ready, 1)

            def x2_stats(b, par, h):
                wait(dve, x2_ready, 2 * b + h + 1)
                if h == 0:
                    wait(dve, ln_rstd, N_TILE + b - 1)
                last = dve.bn_stats(st[:, h, :], x2[par][:, h * 512:(h + 1) * 512])
                if h == 1:
                    last.then_inc(ln_step, 1)
                    ln_settle(N_TILE + b)

            def x2_norm(b, par):
                wait(dve, x2t_done, 2 * b)
                ln_norm(N_TILE + b, par, x2[par][:, :], xn2[:, :], xn2_ready)

            def x2t_out(b, par, r, banks=x2t_bank):
                wait(dve, x2t_hi, 2 * b + r + 1)
                dve.scalar_tensor_tensor(
                    out=xnt[par][:, LO, 4 * r:4 * r + 4, :],
                    in0=banks[r][:, :].rearrange("p (k t) -> p k t", k=4),
                    scalar=FFN_UP, in1=xnt[par][:, HI, 4 * r:4 * r + 4, :],
                    op0=ALU.mult, op1=ALU.subtract).then_inc(x2t_ready, 1)

            def ffn_out(b, par, h):
                wait(dve, ffn_done, 2 * b + h + 1)
                cols = slice(h * 512, (h + 1) * 512)
                dve.scalar_tensor_tensor(out=x2[par][:, cols], in0=ffn_bank[h][:, :], scalar=scale_d[:, 0:1],
                                         in1=x2[par][:, cols], op0=ALU.mult, op1=ALU.add).then_inc(out_ready, 1)

            def unit(b, u, attn, prev):
                pb, pu = (b, u - 1) if u else (b - 1, NKV - 1)
                if attn:
                    row_max(b, u)
                    neg_max(b, u)
                if prev:
                    recip(pb, pu)
                    normalise(pb, pu)

            def step(b, i, par, attn, t1, t2, t3, first=False, second=False):
                for u in range(NKV):
                    if u == (6 if first else 5 if second else 4) and t1:
                        x2_out(b - 1, i - 1 + par, 1 - par, 0)
                        x2_stats(b - 1, 1 - par, 0)
                    if u == 6 and t1 and not first:
                        x2_out(b - 1, i - 1 + par, 1 - par, 1)
                        x2_stats(b - 1, 1 - par, 1)
                        if attn:
                            row_max(b, 6)
                            neg_max(b, 6)
                            recip(b, 5)
                        ln_aggregate(1 - par)
                        if attn:
                            normalise(b, 5)
                            y_out(b, 0)
                        x2_norm(b - 1, 1 - par)
                    else:
                        unit(b, u, attn, t1 if u == 0 else attn)
                    if u == 0 and t2 and not second:
                        x2t_out(b - 2, par, 0)
                        x2t_out(b - 2, par, 1)
                    if u == 0 and t3:
                        ffn_out(b - 3, 1 - par, 0)
                    if u == 7 and first:
                        y_out(b, 0)
                    if u == 0 and first:
                        y_out(b - 1, 0)
                    if u == 1 and second:
                        q_out(N_BLK - 1, NKV - 1)
                        x2_out(b - 2, 0, par, 1)
                    if u == 1 and t1:
                        y_out(b - 1, 1)
                    if u == 1 and t3:
                        ffn_out(b - 3, 1 - par, 1)
                    if u == 1 and second:
                        x2_stats(b - 2, par, 1)
                        ln_aggregate(par)
                    if u == 2 and second:
                        x2_norm(b - 2, par)
                    if u == 3 and second:
                        x2t_out(b - 2, par, 0, x2t_bank0)
                        x2t_out(b - 2, par, 1, x2t_bank0)

            for m in range(NKV // 2 - 1):
                q_out(N_BLK - 1, m)
            dve.wait_ge(const_made, 7)
            for u in range(NKV):
                unit(0, u, True, u > 0)
                if u == 0:
                    q_out(N_BLK - 1, NKV // 2 - 1)
                if u in Q_LO_AT:
                    q_out(N_BLK - 1, Q_LO_AT[u])
            step(1, 0, 1, True, True, False, False, first=True)
            step(2, 1, 0, True, True, True, False, second=True)
            step(3, 1, 1, True, True, True, True)
            with dve.Fori(2, N_BATCH // 2) as i:
                step(2 * i, i, 0, True, True, True, True)
                step(2 * i + 1, i, 1, True, True, True, True)
            step(N_BATCH, N_BATCH // 2, 0, False, True, True, True)
            step(N_BATCH + 1, N_BATCH // 2, 1, False, False, True, True)
            step(N_BATCH + 2, N_BATCH // 2 + 1, 0, False, False, False, True)

        @block.tensor
        def _(pe):
            TERMS = ((HI, HI), (HI, LO), (LO, HI))

            def kv_chunk(n, k, terms=(0, 1, 2)):
                a = act[0]
                for g in range(6):
                    if k == 0:
                        wait(pe, kv_evac, 6 * (n - 1) + g + 1)
                    for p in terms:
                        w_part, a_part = TERMS[p]
                        start, stop = k == 0 and p == 0, k == KC - 1 and p == 2
                        if g < 2:
                            last = pe.matmul(bank[g][:, :], wkv_s[:, k, w_part, g * P:(g + 1) * P],
                                             a[:, k, a_part, :], start=start, stop=stop)
                        else:
                            last = pe.matmul(bank[g][:, 0:KV], a[:, k, w_part, (g - 2) * P:(g - 1) * P],
                                             wkv_s[:, k, a_part, KV:2 * KV], start=start, stop=stop)
                    if k == KC - 1:
                        last.then_inc(kv_done, 1)
                if k < KC - 1 and terms[-1] == 2:
                    last.then_inc(c_used, 1)

            def transpose_x(i):
                wait(pe, xn_ready, i + 1)
                for r in range(2):
                    wait(pe, xt_ready, 2 * (i - 1) + r + 1)
                    for k in range(4):
                        c = 4 * r + k
                        last = pe.transpose(x_t[r][:, k * P:(k + 1) * P],
                                            x_raw[i % XRING][:, c * P:(c + 1) * P], ident[:, :])
                    last.then_inc(xt_done, 1)

            def q_chunks(n, m, k0, k1):
                if k0 == 0:
                    wait(pe, q_evac, NKV * n + m - 3)
                    if n == 0 and m < 4:
                        wait(pe, kv_evac, 6 * (N_BLK - 1) + m + 1)
                for k in range(k0, k1):
                    for p, (w_part, a_part) in enumerate(((HI, HI), (HI, LO), (LO, HI))):
                        last = pe.matmul(bank[m % 4][:, :], wq_s[:, m, k, w_part, :],
                                         act_of(n)[:, k, a_part, :], start=k == 0 and p == 0,
                                         stop=k == KC - 1 and p == 2)
                if k1 == KC:
                    last.then_inc(q_done, 1)

            pe.wait_ge(c_hi, 1)
            pe.wait_ge(wkv_hi, 1)
            kv_chunk(0, 0, (0,))
            for k in range(KC):
                wait(pe, c_ready, k + 1)
                wait(pe, wkv_ready, k + 1)
                kv_chunk(0, k, (1, 2) if k == 0 else (0, 1, 2))
            with pe.Fori(1, N_BLK - 1) as n:
                for k in range(KC):
                    wait(pe, c_ready, KC * n + k + 1)
                    kv_chunk(n, k)
            pe.wait_ge(const_made, 6)
            for k in range(KC):
                wait(pe, c_ready, KC * (N_BLK - 1) + k + 1)
                kv_chunk(N_BLK - 1, k)
                if 3 <= k < 3 + TPB:
                    transpose_x(k - 3)
            pe.wait_ge(wq_ready, KC)
            for n in range(N_BLK - 1):
                wait(pe, xt_ready, 2 * TPB * (n + 1))
                for m in range(NKV):
                    q_chunks(n, m, 0, KC)
                    if m % 2 == 0:
                        transpose_x(TPB * (n + 1) + m // 2)

            def scores(b, i, par, u):
                if u == 0:
                    wait(pe, qv_loaded[par], 9 * 16 * (i + 1))
                if u % 4 == 0:
                    wait(pe, kd_loaded[u // 4], 4 * 16 * (b + 1))
                wait(pe, exp_done, NKV * b + u - 1)
                for pair in range(2):
                    for k_part in (HI, LO):
                        last = pe.matmul(score[u % 2][:, pair * 2 * P:(pair + 1) * 2 * P],
                                         q_s[par][:, u, pair, :], kd[:, u, k_part, :],
                                         start=k_part == HI, stop=k_part == LO)
                last.then_inc(qk_done, 1)

            def transpose_p(b, u):
                wait(pe, prob_ready, NKV * b + u + 1)
                wait(pe, pt_ready, NKV * b + u - 1)
                for g in range(G):
                    last = pe.transpose(prob_t[u % 2][:, g * P:(g + 1) * P], pr[u % 2][:, g, :], ident[:, :])
                last.then_inc(tp_done, 1)

            def attend(b, par, half, x2t_count=None):
                wait(pe, pt_ready, NKV * b + 4 * half + 4)
                wait(pe, y_ready, 2 * b + half)
                if x2t_count is not None:
                    wait(pe, x2t_ready, x2t_count)
                for c in range(4):
                    u = 4 * half + c
                    last = pe.matmul(y_bank[c * HD:(c + 1) * HD, :], v_s[par][:, u * HD:(u + 1) * HD],
                                     pt[:, u, :], start=True, stop=True)
                last.then_inc(pv_done, 1)

            def project(b, s0, s1):
                for s in range(s0, s1):
                    h, k = s // KC, s % KC
                    if s == 0:
                        wait(pe, y_ready, 2 * b + 1)
                        if isinstance(b, int) and b == 1:
                            wait(pe, x2_ready, 1)
                        else:
                            wait(pe, x2t_ready, 2 * b - 1)
                    if s == 4:
                        wait(pe, y_ready, 2 * b + 2)
                    if s == KC:
                        wait(pe, x2_ready, 2 * b)
                        wait(pe, out_ready, 2 * (b - 2) + 2)
                    for p, (y_part, w_part) in enumerate(((HI, HI), (HI, LO), (LO, HI))):
                        last = pe.matmul(o_bank[h][:, :], yt[:, k, y_part, :],
                                         wo_chunk(k, w_part)[:, h * 512:(h + 1) * 512],
                                         start=k == 0 and p == 0, stop=k == KC - 1 and p == 2)
                    if k == KC - 1:
                        last.then_inc(o_done, 1)
                return last

            def transpose_x2(b, y_count, banks=x2t_bank):
                wait(pe, xn2_ready, b + 1)
                wait(pe, y_ready, y_count)
                for r in range(2):
                    for k in range(4):
                        c = 4 * r + k
                        last = pe.transpose(banks[r][:, k * P:(k + 1) * P],
                                            xn2[:, c * P:(c + 1) * P], ident[:, :])
                    last.then_inc(x2t_done, 1)

            def ffn(b, par, s0, s1, projecting):
                for s in range(s0, s1):
                    h, k = s // KC, s % KC
                    if s == 0:
                        wait(pe, x2t_ready, 2 * b + 2)
                        wait(pe, out_ready, 2 * (b - 1) + 1)
                    if s == KC:
                        if projecting:
                            wait(pe, x2_ready, 2 * (b + 1) + 2)
                        else:
                            wait(pe, out_ready, 2 * (b - 1) + 2)
                    for part in (HI, LO):
                        last = pe.matmul(ffn_bank[h][:, :], xnt[par][:, part, k, :],
                                         ffn_s[:, k, h * 512:(h + 1) * 512],
                                         start=k == 0 and part == HI, stop=k == KC - 1 and part == LO)
                    if k == KC - 1:
                        last.then_inc(ffn_done, 1)

            O_AT = {1: (0, 3), 2: (3, 7), 3: (7, 10), 4: (10, 13), 5: (13, 16)}
            FFN_HEAD = 10
            O_AT_FIRST = {1: (0, 2), 2: (2, 4), 3: (4, 6), 4: (6, 7), 5: (7, 9), 6: (9, 12)}
            O_HEAD = 12

            def q_share(c0, c1):
                for c in range(c0, c1):
                    q_chunks(N_BLK - 1, NKV // 2 + c // KC, c % KC, c % KC + 1)

            def opening(b, i, par, t1, t3, first, second):
                if first:
                    q_share(Q_END[-1], Q_LATE[0][0])
                    pe.wait_ge(q_evac, NKV * N_BLK - 1)
                    attend(b - 1, 1 - par, 0)
                if second:
                    project(b - 2, O_HEAD, 2 * KC)
                if t3:
                    ffn(b - 3, 1 - par, FFN_HEAD, 2 * KC, t1)

            def step(b, i, par, attn, t1, t2, t3, first=False, second=False, more=True):
                o_at = O_AT_FIRST if first else O_AT
                for u in range(NKV):
                    if u == 0:
                        opening(b, i, par, t1, t3, first, second)
                    if u in Q_LATE and first:
                        q_share(*Q_LATE[u])
                    if u == 1 and first:
                        pe.wait_ge(wo_ready, KC)
                    if u == 1 and t1:
                        s0, s1 = o_at[u]
                        middle = (s0 + s1 + 1) // 2
                        project(b - 1, s0, middle)
                        attend(b - 1, 1 - par, 1, None if first or second else 2 * (b - 1))
                        project(b - 1, middle, s1)
                    elif u in o_at and t1:
                        last = project(b - 1, *o_at[u])
                        if first and o_at[u][1] == O_HEAD:
                            last.then_inc(y0_used, 1)
                    if u == 3 and second:
                        pe.wait_ge(q_evac, NKV * N_BLK)
                        transpose_x2(b - 2, 2 * b, x2t_bank0)
                    if u == 6 and t2:
                        if second:
                            pe.wait_ge(ffn_ready, KC)
                        ffn(b - 2, par, 0, 5, t1)
                    if u == 7:
                        if t2:
                            ffn(b - 2, par, 5, 7, t1)
                        if t1 and not first:
                            transpose_x2(b - 1, 2 * b + (1 if attn else 0))
                        if t2:
                            ffn(b - 2, par, 7, FFN_HEAD if t1 else 2 * KC, t1)
                    if attn and u < NKV - 1:
                        scores(b, i, par, u + 1)
                    elif attn and more:
                        scores(b + 1, i + par, 1 - par, 0)
                    if u == 0 and t1:
                        transpose_p(b - 1, 7)
                    if u and attn:
                        transpose_p(b, u - 1)
                    if u == 5 and attn:
                        attend(b, par, 0, 2 if second else None)

            wait(pe, xt_ready, 2 * N_TILE)
            for m in range(NKV // 2 - 1):
                q_chunks(N_BLK - 1, m, 0, KC)
            pe.wait_ge(kd_zeroed, 2)
            scores(0, 0, 0, 0)
            q_chunks(N_BLK - 1, NKV // 2 - 1, 0, KC)
            for u in range(NKV):
                q_share(Q_END[u - 1] if u else 0, Q_END[u])
                if u < NKV - 1:
                    scores(0, 0, 0, u + 1)
                else:
                    scores(1, 0, 1, 0)
                if u:
                    transpose_p(0, u - 1)
            step(1, 0, 1, True, True, False, False, first=True)
            step(2, 1, 0, True, True, True, False, second=True)
            step(3, 1, 1, True, True, True, True)
            last_pair = N_BATCH // 2 - 1
            with pe.Fori(2, last_pair) as i:
                step(2 * i, i, 0, True, True, True, True)
                step(2 * i + 1, i, 1, True, True, True, True)
            step(N_BATCH - 2, last_pair, 0, True, True, True, True)
            step(N_BATCH - 1, last_pair, 1, True, True, True, True, more=False)
            step(N_BATCH, N_BATCH // 2, 0, False, True, True, True)
            step(N_BATCH + 1, N_BATCH // 2, 1, False, False, True, True)


def kernel(x, ctx_4096, L0_xattn_Wq, L0_xattn_bq, L0_xattn_Wk, L0_xattn_bk, L0_xattn_Wv, L0_xattn_bv,
           L0_xattn_Wo, L0_xattn_bo, L0_ffn_kernel, L0_ffn_scale):
    import numpy as np
    import concourse.bacc as bacc
    from concourse.bass_utils import run_bass_kernel_spmd

    wo_rows = np.asarray(L0_xattn_Wo).reshape(2, 4, G, HD, D).transpose(0, 2, 1, 3, 4).reshape(D, D)
    arrays = {
        "x": np.asarray(x).reshape(N_BATCH * P, D),
        "ctx_t": np.asarray(ctx_4096).reshape(N_BATCH * P, D).T,
        "wq": np.asarray(L0_xattn_Wq),
        "bq": np.asarray(L0_xattn_bq).reshape(KC, P).T,
        "wkv": np.concatenate([np.asarray(L0_xattn_Wk), np.asarray(L0_xattn_Wv)], axis=1),
        "bk": np.asarray(L0_xattn_bk).reshape(2, P).T,
        "bv": np.asarray(L0_xattn_bv),
        "wo": wo_rows,
        "bo": np.asarray(L0_xattn_bo),
        "ffn_w": np.asarray(L0_ffn_kernel),
        "ffn_scale": np.asarray(L0_ffn_scale).reshape(1),
    }
    arrays = {n: np.ascontiguousarray(a) for n, a in arrays.items()}
    nc = bacc.Bacc("TRN2", target_bir_lowering=False, num_devices=1)
    args = [nc.dram_tensor(n, a.shape, mybir.dt.from_np(a.dtype), kind="ExternalInput").ap()
            for n, a in arrays.items()]
    out = nc.dram_tensor("out", (N_BATCH * P, D), F32, kind="ExternalOutput").ap()
    attention_ffn(nc, *args, out)
    r = run_bass_kernel_spmd(nc, [arrays], core_ids=[0])
    return np.asarray(r.results[0]["out"]).reshape(N_BATCH, P, D)
```
